# Optimizing a Trainium2 kernel written in Bass

```python
import numpy as np
import jax
import jax.numpy as jnp

def _softmax(x, axis=-1):
    return jax.nn.softmax(x, axis=axis)

def _gelu(x):
    return jax.nn.gelu(x, approximate=True)

def _silu(x):
    return jax.nn.silu(x)

def _sigmoid(x):
    return jax.nn.sigmoid(x)

def _layernorm(x, axis=-1, eps=1e-05):
    m = jnp.mean(x, axis=axis, keepdims=True)
    v = jnp.var(x, axis=axis, keepdims=True)
    return (x - m) / jnp.sqrt(v + eps)

def _scatter_add(tgt, idx, src, axis=0):
    return tgt.at[idx].add(src)

def _segment_sum(src, seg, n):
    return jax.ops.segment_sum(src, seg, n)
kernel_name = 'mk_seq_postln_d1_jaxref_r4_00a8a4'

def setup_inputs(seed: int=0):
    np.random.seed(seed)
    _w = jnp.asarray

    def _L0_attn_setup():
        import jax, jax.numpy as jnp
        import numpy as np
        import math
        D_MODEL = 1024
        NUM_HEADS = 32
        NUM_KV_HEADS = 8
        HEAD_DIM = D_MODEL // NUM_HEADS
        GROUP = NUM_HEADS // NUM_KV_HEADS
        SEQ_LEN = 512
        BATCH = 2
        ROPE_THETA = 10000.0

        def apply_rope(x, start_pos=0):
            b, h, s, hd = x.shape
            inv_freq = 1.0 / ROPE_THETA ** (jnp.arange(0, hd, 2, dtype=jnp.float32) / hd)
            pos = jnp.arange(start_pos, start_pos + s, dtype=jnp.float32)
            ang = pos[:, None] * inv_freq[None, :]
            cos = jnp.cos(ang).astype(x.dtype)
            sin = jnp.sin(ang).astype(x.dtype)
            xr = x[..., 0::2]
            xi = x[..., 1::2]
            out_r = xr * cos - xi * sin
            out_i = xr * sin + xi * cos
            return jnp.stack([out_r, out_i], axis=-1).reshape(b, h, s, hd)
        key = jax.random.key(seed)
        ks = jax.random.split(key, 5)
        qkv_dim = HEAD_DIM * (NUM_HEADS + 2 * NUM_KV_HEADS)
        scale = 1.0 / math.sqrt(D_MODEL)
        return {'x': jax.random.normal(ks[0], (BATCH, SEQ_LEN, D_MODEL), jnp.float32), 'w_qkv': jax.random.normal(ks[1], (qkv_dim, D_MODEL), jnp.float32) * scale, 'b_qkv': jax.random.normal(ks[2], (qkv_dim,), jnp.float32) * 0.01, 'w_o': jax.random.normal(ks[3], (D_MODEL, D_MODEL), jnp.float32) * scale, 'b_o': jax.random.normal(ks[4], (D_MODEL,), jnp.float32) * 0.01}
    _L0_attn_in = _L0_attn_setup()

    def _L0_ffn_setup():
        import jax, jax.numpy as jnp
        import numpy as np
        B, L, H, Dh, M = (4, 512, 16, 64, 256)
        D = H * Dh
        key = jax.random.key(seed)
        kx, ku, kd, kp = jax.random.split(key, 4)
        x = jax.random.normal(kx, (B, L, D), dtype=jnp.float32)
        up = jax.random.normal(ku, (H, Dh, M), dtype=jnp.float32)
        down = jax.random.normal(kd, (H, M, Dh), dtype=jnp.float32)
        perm = jax.random.permutation(kp, D)
        return {'x': x, 'up': up, 'down': down, 'perm': perm}
    _L0_ffn_in = _L0_ffn_setup()
    _d = {'L0_attn_x': _L0_attn_in['x'], 'L0_attn_w_qkv': _L0_attn_in['w_qkv'], 'L0_attn_b_qkv': _L0_attn_in['b_qkv'], 'L0_attn_w_o': _L0_attn_in['w_o'], 'L0_attn_b_o': _L0_attn_in['b_o'], 'L0_ffn_up': _L0_ffn_in['up'], 'L0_ffn_down': _L0_ffn_in['down'], 'L0_ffn_perm': _L0_ffn_in['perm']}
    _x0 = _d['L0_attn_x']
    _d['L0_attn_x'] = jax.random.normal(jax.random.fold_in(jax.random.key(seed), 1), (2, 2048, 1024), dtype=_x0.dtype)
    del _x0
    return _d

def reference(L0_attn_x, L0_attn_w_qkv, L0_attn_b_qkv, L0_attn_w_o, L0_attn_b_o, L0_ffn_up, L0_ffn_down, L0_ffn_perm):

    def _L0_attn_ref(x, w_qkv, b_qkv, w_o, b_o):
        import jax, jax.numpy as jnp
        import numpy as np
        import math
        D_MODEL = 1024
        NUM_HEADS = 32
        NUM_KV_HEADS = 8
        HEAD_DIM = D_MODEL // NUM_HEADS
        GROUP = NUM_HEADS // NUM_KV_HEADS
        SEQ_LEN = 512
        BATCH = 2
        ROPE_THETA = 10000.0

        def apply_rope(x, start_pos=0):
            b, h, s, hd = x.shape
            inv_freq = 1.0 / ROPE_THETA ** (jnp.arange(0, hd, 2, dtype=jnp.float32) / hd)
            pos = jnp.arange(start_pos, start_pos + s, dtype=jnp.float32)
            ang = pos[:, None] * inv_freq[None, :]
            cos = jnp.cos(ang).astype(x.dtype)
            sin = jnp.sin(ang).astype(x.dtype)
            xr = x[..., 0::2]
            xi = x[..., 1::2]
            out_r = xr * cos - xi * sin
            out_i = xr * sin + xi * cos
            return jnp.stack([out_r, out_i], axis=-1).reshape(b, h, s, hd)
        bs, seq_len, d_model = x.shape
        qkv = x @ w_qkv.T + b_qkv
        q_dim = NUM_HEADS * HEAD_DIM
        kv_dim = NUM_KV_HEADS * HEAD_DIM
        q, k, v = jnp.split(qkv, [q_dim, q_dim + kv_dim], axis=-1)
        q = q.reshape(bs, seq_len, NUM_HEADS, HEAD_DIM).transpose(0, 2, 1, 3)
        k = k.reshape(bs, seq_len, NUM_KV_HEADS, HEAD_DIM).transpose(0, 2, 1, 3)
        v = v.reshape(bs, seq_len, NUM_KV_HEADS, HEAD_DIM).transpose(0, 2, 1, 3)
        q = apply_rope(q, 0)
        k = apply_rope(k, 0)
        k = jnp.repeat(k, GROUP, axis=1)
        v = jnp.repeat(v, GROUP, axis=1)
        scores = jnp.einsum('bhqd,bhkd->bhqk', q, k) / math.sqrt(HEAD_DIM)
        causal = jnp.tril(jnp.ones((seq_len, seq_len), dtype=bool))
        scores = jnp.where(causal[None, None, :, :], scores, jnp.float32(-1e+20))
        attn = jax.nn.softmax(scores, axis=-1)
        out = jnp.einsum('bhqk,bhkd->bhqd', attn, v)
        out = out.transpose(0, 2, 1, 3).reshape(bs, seq_len, d_model)
        return out @ w_o.T + b_o

    def _L0_ffn_ref(x, up, down, perm):
        import jax, jax.numpy as jnp
        import numpy as np
        B, L, H, Dh, M = (4, 512, 16, 64, 256)
        D = H * Dh
        b, l, Dm = x.shape
        h, d = (up.shape[0], up.shape[1])
        unperm = jnp.argsort(perm)
        t = x.reshape(b * l, Dm)
        t = t[:, perm]
        t = t.reshape(b * l, h, d)
        t = jnp.einsum('bhd,hdm->bhm', t, up)
        t = jax.nn.gelu(t, approximate=False)
        t = jnp.einsum('bhm,hmd->bhd', t, down)
        t = t.reshape(b * l, h * d)
        t = t[:, unperm]
        out = t.reshape(b, l, Dm)
        return out
    x = L0_attn_x
    x = _layernorm(x + _L0_attn_ref(x, L0_attn_w_qkv, L0_attn_b_qkv, L0_attn_w_o, L0_attn_b_o), axis=-1)
    x = _layernorm(x + _L0_ffn_ref(x, L0_ffn_up, L0_ffn_down, L0_ffn_perm), axis=-1)
    return x

_drawn_inputs = setup_inputs


def setup_inputs(seed=0):
    import zlib

    import numpy as np

    out = dict(_drawn_inputs(seed))
    spreads = {}
    factors = {'L0_attn_b_qkv': 4.73, 'L0_attn_b_o': 5.895}
    for name, (base, spread) in spreads.items():
        noise = np.random.default_rng([zlib.crc32(name.encode()), seed]).standard_normal(out[name].shape)
        drawn = base * np.exp(spread * noise) if base else spread * noise
        out[name] = jnp.asarray(drawn.astype(out[name].dtype))
    for name, factor in factors.items():
        out[name] = (out[name] * factor).astype(out[name].dtype)
    return out
```

```python
from contextlib import ExitStack

import concourse.bass as bass
import numpy as np
from concourse import mybir
from concourse.alu_op_type import AluOpType as ALU

F32 = mybir.dt.float32
F32R = mybir.dt.float32r
I32 = mybir.dt.int32
U32 = mybir.dt.uint32
ACT = mybir.ActivationFunctionType
AX = mybir.AxisListType

P = 128
B, S, D = 2, 2048, 1024
T = B * S
H, KV, HD = 32, 8, 32
HALF = HD // 2
CH = 512
NCH = T // CH
CPB = S // CH
KT = D // P
NKV = KV * HD
QK_PAIRS = (H + KV) * HALF // P
HPT = P // HALF
EPS = 1e-5
LOWEST = -3.0e38
FH, FD, FM = 16, 64, 256
DMA = 16


def ds(start, size):
    return bass.ds(start, size)


def wait_apart(eng, sem, value, passed):
    eng.wait_ge(sem, value)
    eng.sem_inc(passed, 1)


def project(nc, xT, wqkvT, bias_qk, bias_v, cos, sin, qk_halves, v_keys):
    with ExitStack() as ctx:
        def sb(name, shape, dt):
            return ctx.enter_context(nc.sbuf_tensor(name, shape, dt))

        def sem(name):
            return ctx.enter_context(nc.semaphore(name))

        NW = 2 * QK_PAIRS * P + NKV
        w_hi = sb("w_hi", [P, KT, NW], F32R)
        w_lo = sb("w_lo", [P, KT, NW], F32R)
        x_in = sb("x_in", [P, KT, CH], F32)
        w_in = x_in[:, 0:6, :].rearrange("p a c -> p (a c)").rearrange("p (s n) -> p s n", s=2)
        x_hi = sb("x_hi", [P, 2, KT, CH], F32R)
        x_lo = sb("x_lo", [P, 2, KT, CH], F32R)
        trig = sb("trig", [P, 2, CH], F32)
        prod = sb("prod", [P, 4, CH], F32)
        rot = prod[:, 0:2, :]
        halves = sb("halves", [P, 4, CH], F32R)
        v_out = sb("v_out", [P, 2, NKV], F32)
        bqk = sb("bqk", [P, 2 * QK_PAIRS], F32)
        bv = sb("bv", [P, NKV], F32)
        ps_qk = ctx.enter_context(nc.psum_tensor("ps_qk", [P, 2, 2, CH], F32))
        ps_v = ctx.enter_context(nc.psum_tensor("ps_v", [P, 2, CH], F32))

        bias_in = sem("bias_in")
        w_loaded = [sem(f"w_loaded{i}") for i in range(2)]
        w_hi_done = sem("w_hi_done")
        w_split = sem("w_split")
        x_loaded = sem("x_loaded")
        x_hi_done = sem("x_hi_done")
        x_split = sem("x_split")
        trig_loaded = sem("trig_loaded")
        qk_ready = sem("qk_ready")
        rope_mul = sem("rope_mul")
        rope_sum = sem("rope_sum")
        rope_hi = sem("rope_hi")
        rope_lo = sem("rope_lo")
        qk_stored = sem("qk_stored")
        v_ready = sem("v_ready")
        v_added = sem("v_added")
        v_stored = [sem(f"v_stored{i}") for i in range(2)]
        block = ctx.enter_context(nc.Block())
        ITER = NCH // 2

        @block.sync
        def _(sp):
            sp.dma_start(bqk[:, :], bias_qk).then_inc(bias_in, DMA)
            sp.dma_start(bv[:, :], bias_v.rearrange("(a n) -> a n", a=1).to_broadcast([P, NKV])).then_inc(bias_in, DMA)
            for k in range(KT):
                if k >= 2:
                    sp.wait_ge(w_split, k - 1)
                sp.dma_start(w_in[:, k % 2, :], wqkvT[k * P:(k + 1) * P, :]).then_inc(w_loaded[k % 2], DMA)
            sp.sem_inc(qk_stored, 4 * DMA)
            for i in range(2):
                sp.sem_inc(v_stored[i], DMA)
            sp.wait_ge(x_split, 1)
            sp.dma_start(x_in[:, :, :], xT[:, 0:CH].rearrange("(k p) t -> p k t", p=P)).then_inc(x_loaded, DMA)
            with sp.Fori(0, ITER) as it:
                for u in range(2):
                    c = it * 2 + u
                    tok = (c % CPB) * CH
                    sp.wait_ge(rope_mul, c * QK_PAIRS + 2)
                    sp.dma_start(trig[:, 0, :], cos[:, ds(tok, CH)]).then_inc(trig_loaded, DMA)
                    sp.dma_start(trig[:, 1, :], sin[:, ds(tok, CH)]).then_inc(trig_loaded, DMA)
                    sp.wait_ge(x_split, c + 2)
                    sp.dma_start(x_in[:, :, :], xT[:, ds(((c + 1) % NCH) * CH, CH)]
                                 .rearrange("(k p) t -> p k t", p=P)).then_inc(x_loaded, DMA)
                    for j in range(QK_PAIRS):
                        sp.wait_ge(rope_lo, c * QK_PAIRS + j + 2)
                        for v in range(4):
                            sp.dma_start(qk_halves[ds(c // CPB, 1), j * HPT:(j + 1) * HPT, v, :, ds(tok, CH)]
                                         .rearrange("b h i t -> (b h) i t"),
                                         halves[:, v, :].bitcast(F32)).then_inc(qk_stored, DMA)
                    for t in range(CH // P):
                        sp.wait_ge(v_added, c * 4 + t + 5)
                        sp.dma_start(v_keys[ds(c // CPB, 1), :, :, ds((c % CPB) * 4 + t, 1), :]
                                     .rearrange("b g p k d -> p (b g) (k d)"),
                                     v_out[:, t % 2, :].rearrange("p (g d) -> p g d", d=HD)).then_inc(v_stored[t % 2], DMA)
            sp.wait_ge(qk_stored, 4 * DMA * (NCH * QK_PAIRS + 1))
            for i in range(2):
                sp.wait_ge(v_stored[i], DMA * (NCH * 2 + 1))
            sp.wait_ge(x_loaded, DMA * (NCH + 1))

        @block.scalar
        def _(act):
            for k in range(KT):
                act.wait_ge(w_loaded[k % 2], DMA * (k // 2 + 1))
                act.activation(w_hi[:, k, :], w_in[:, k % 2, :], ACT.Copy).then_inc(w_hi_done, 1)

            def split_x(c, u):
                act.wait_ge(x_loaded, (c + 1) * DMA)
                act.wait_ge(v_ready, c * 2)
                act.activation(x_hi[:, u, :, :], x_in[:, :, :], ACT.Copy).then_inc(x_hi_done, 1)

            act.wait_ge(x_loaded, DMA)
            act.activation(x_hi[:, 0, :, :], x_in[:, :, :], ACT.Copy).then_inc(x_hi_done, 1)
            with act.Fori(0, ITER) as it:
                for u in range(2):
                    c = it * 2 + u
                    for j in range(QK_PAIRS):
                        n = c * QK_PAIRS + j
                        if j == 2:
                            split_x(c + 1, 1 - u)
                        act.wait_ge(rope_sum, 2 * n + 2)
                        act.wait_ge(qk_stored, (n + 1) * 4 * DMA)
                        act.activation(halves[:, 0:2, :], rot, ACT.Copy).then_inc(rope_hi, 1)

        @block.gpsimd
        def _(pool):
            pool.sem_inc(rope_lo, 1)
            with pool.Fori(0, ITER) as it:
                for u in range(2):
                    for j in range(QK_PAIRS):
                        n = (it * 2 + u) * QK_PAIRS + j
                        pool.wait_ge(rope_mul, n + 3)
                        pool.tensor_tensor(prod[:, 0, :], prod[:, 0, :], prod[:, 2, :], ALU.subtract).then_inc(rope_sum, 1)
                        pool.tensor_tensor(prod[:, 1, :], prod[:, 1, :], prod[:, 3, :], ALU.add).then_inc(rope_sum, 1)
                        pool.wait_ge(rope_hi, n + 1)
                        pool.tensor_tensor(halves[:, 2:4, :], rot, halves[:, 0:2, :].bitcast(F32), ALU.subtract).then_inc(rope_lo, 1)

        @block.vector
        def _(dve):
            dve.sem_inc(rope_mul, 2)
            dve.sem_inc(v_added, 4)
            for k in range(KT):
                dve.wait_ge(w_hi_done, k + 1)
                ins = dve.tensor_tensor(w_lo[:, k, :], w_in[:, k % 2, :], w_hi[:, k, :].bitcast(F32), ALU.subtract)
                ins.then_inc(w_split, 1)
            dve.wait_ge(w_split, KT)
            dve.sem_inc(x_split, 1)
            dve.wait_ge(bias_in, 2 * DMA)

            def split_x(c, u):
                dve.wait_ge(x_hi_done, c + 1)
                dve.tensor_tensor(x_lo[:, u, :, :], x_in[:, :, :], x_hi[:, u, :, :].bitcast(F32), ALU.subtract).then_inc(x_split, 1)

            dve.wait_ge(x_hi_done, 1)
            dve.tensor_tensor(x_lo[:, 0, :, :], x_in[:, :, :], x_hi[:, 0, :, :].bitcast(F32), ALU.subtract).then_inc(x_split, 1)
            with dve.Fori(0, ITER) as it:
                for u in range(2):
                    c = it * 2 + u
                    for j in range(QK_PAIRS):
                        n = c * QK_PAIRS + j
                        if j == 3:
                            split_x(c + 1, 1 - u)
                        if j == 0:
                            dve.wait_ge(trig_loaded, (c + 1) * 2 * DMA)
                        dve.wait_ge(qk_ready, n + 1)
                        dve.wait_ge(rope_lo, n + 1)
                        for k, (part, table) in enumerate(((0, 0), (1, 0), (1, 1), (0, 1))):
                            ins = dve.scalar_tensor_tensor(
                                out=prod[:, k, :], in0=ps_qk[:, j % 2 if u == 0 else (j + QK_PAIRS) % 2, part, :],
                                scalar=bqk[:, 2 * j + part:2 * j + part + 1], in1=trig[:, table, :],
                                op0=ALU.add, op1=ALU.mult)
                        ins.then_inc(rope_mul, 1)
                    for t in range(CH // P):
                        if t % 2 == 0:
                            dve.wait_ge(v_ready, c * 2 + t // 2 + 3)
                        dve.wait_ge(v_stored[t % 2], (c * 2 + t // 2 + 1) * DMA)
                        dve.tensor_tensor(v_out[:, t % 2, :], ps_v[:, t // 2, (t % 2) * NKV:(t % 2 + 1) * NKV],
                                          bv[:, :], ALU.add).then_inc(v_added, 1)

        @block.tensor
        def _(pe):
            pe.sem_inc(v_ready, 2)
            pe.wait_ge(w_split, KT)
            with pe.Fori(0, ITER) as it:
                for u in range(2):
                    c = it * 2 + u
                    pe.wait_ge(x_split, c + 2)
                    for j in range(QK_PAIRS):
                        n = c * QK_PAIRS + j
                        pe.wait_ge(rope_mul, n + 1)
                        for part in range(2):
                            cols = slice((2 * j + part) * P, (2 * j + part + 1) * P)
                            terms = [(w, x, k) for k in range(KT) for w, x in ((w_hi, x_hi), (w_hi, x_lo), (w_lo, x_hi))]
                            for i, (w, x, k) in enumerate(terms):
                                ins = pe.matmul(ps_qk[:, j % 2 if u == 0 else (j + QK_PAIRS) % 2, part, :], w[:, k, cols], x[:, u, k, :],
                                                start=(i == 0), stop=(i == len(terms) - 1))
                        ins.then_inc(qk_ready, 1)
                    for t in range(CH // P):
                        if t % 2 == 0:
                            pe.wait_ge(v_added, c * 4 + t + 2)
                        cols = slice(2 * QK_PAIRS * P, NW)
                        terms = [(w, x, k) for k in range(KT) for w, x in ((w_hi, x_hi), (w_lo, x_hi), (w_hi, x_lo))]
                        for i, (w, x, k) in enumerate(terms):
                            ins = pe.matmul(ps_v[:, t // 2, (t % 2) * NKV:(t % 2 + 1) * NKV],
                                            x[:, u, k, t * P:(t + 1) * P], w[:, k, cols],
                                            start=(i == 0), stop=(i == len(terms) - 1))
                        if t % 2 == 1:
                            ins.then_inc(v_ready, 1)


QT = S // P
SLOTS = 2
NPAIR = B * H // 2
STEPS = [(c, kt) for c in range(CPB) for kt in range((c + 1) * CH // P)]
NSTEP = len(STEPS)
CHUNK_END = [STEPS.index((c, (c + 1) * CH // P - 1)) + 1 for c in range(CPB)]
UNITS = [(j, t, g) for t in range(QT) for g in range(t * P // CH + 1) for j in range(2)]
NUNIT = len(UNITS) + 2
ROWS = 3 * HD
RING = 4
FIRST_UNIT, PER_STEP, TRANSPOSE_AT = 4, 3, 34


def unit_slots():
    slots, n = [[] for _ in STEPS], 0
    for i in range(FIRST_UNIT, NSTEP):
        while n < len(UNITS) and len(slots[i]) < PER_STEP:
            slots[i].append(n)
            n += 1
    assert n == len(UNITS) and max(i for i, x in enumerate(slots) if x) < TRANSPOSE_AT - 1
    slots[TRANSPOSE_AT] += [n, n + 1]
    return slots


def attend(nc, qk_halves, v_keys, identity, att_o, att_l):
    with ExitStack() as ctx:
        def sb(name, shape, dt):
            return ctx.enter_context(nc.sbuf_tensor(name, shape, dt))

        def sem(name):
            return ctx.enter_context(nc.semaphore(name))

        q_st = sb("q_st", [P, SLOTS, 2, S], F32R)
        k_st = sb("k_st", [P, SLOTS, S], F32R)
        v_st = sb("v_st", [P, SLOTS, QT, 2 * HD], F32)
        probs = sb("probs", [P, RING, 2, CH], F32)
        o_sb = sb("o_sb", [P, 2, CH], F32)
        ident = sb("ident", [P, P], F32)
        causal = sb("causal", [P, CH], F32)
        scratch = sb("scratch", [P, 2, CH], F32)
        part_max = sb("part_max", [P, 2, QT, CPB], F32)
        neg_max = sb("neg_max", [P, 2, QT], F32)
        max_halves = sb("max_halves", [P, 2, 2, QT], F32R)
        max_rows = sb("max_rows", [2 * QT, 2, P], F32R)
        ps_s = ctx.enter_context(nc.psum_tensor("ps_s", [P, 2, 2, CH], F32))
        ps_o = ctx.enter_context(nc.psum_tensor("ps_o", [P, 2, CH], F32))
        ps_m = ctx.enter_context(nc.psum_tensor("ps_m", [P, 2, CH], F32))

        causal_ready = sem("causal_ready")
        ones_ready = sem("ones_ready")
        ident_in = sem("ident_in")
        q_loaded = [sem(f"q_loaded{i}") for i in range(SLOTS)]
        kv_loaded = [sem(f"kv_loaded{i}") for i in range(SLOTS)]
        s_ready = sem("s_ready")
        exp_done = sem("exp_done")
        masked = sem("masked")
        pv_done = sem("pv_done")
        o_copied = sem("o_copied")
        o_stored = [sem(f"o_stored{i}") for i in range(2)]
        m_ready = sem("m_ready")
        m_used = sem("m_used")
        max_step = sem("max_step")
        rows_loaded = sem("rows_loaded")
        dve_passed = sem("dve_passed")
        pool_passed = sem("pool_passed")
        block = ctx.enter_context(nc.Block())
        slots_of_units = unit_slots()
        NDIAG = CPB * (CH // P)

        def stages(eng, stage):
            with eng.Fori(0, NPAIR // 2 - 1) as it:
                for s in range(SLOTS):
                    stage(it, s, True)
            stage(NPAIR // 2 - 1, 0, True)
            stage(NPAIR // 2 - 1, 1, False)

        @block.sync
        def _(sp):
            def where(it, s):
                return it // KV, it % KV, (it % KV) * 4 + 2 * s

            def load_q(it, s, c):
                b, _, h = where(it, s)
                for j in range(2):
                    head = qk_halves[ds(b, 1), ds(h + j, 1), :, :, c * CH:(c + 1) * CH].rearrange("b h v i t -> (b h v i) t")
                    sp.dma_start(q_st[0:HD, s, j, c * CH:(c + 1) * CH].bitcast(F32), head[0:HD, :]).then_inc(q_loaded[s], DMA)
                    sp.dma_start(q_st[HD:3 * HD, s, j, c * CH:(c + 1) * CH].bitcast(F32), head).then_inc(q_loaded[s], DMA)

            def load_kv(it, s):
                b, g, _ = where(it, s)
                head = qk_halves[ds(b, 1), ds(g + H, 1)].rearrange("b h v i t -> (b h v i) t")
                sp.dma_start(k_st[0:2 * HD, s, :].bitcast(F32), head).then_inc(kv_loaded[s], DMA)
                sp.dma_start(k_st[2 * HD:3 * HD, s, :].bitcast(F32), head[0:HD, :]).then_inc(kv_loaded[s], DMA)
                sp.dma_start(v_st[:, s, :, 0:HD], v_keys[ds(b, 1), ds(g, 1)].rearrange("b g p k d -> (b g p) k d")).then_inc(kv_loaded[s], DMA)

            def load_rows(it, s, p):
                sp.wait_ge(m_used, (p + 1) * NUNIT + 2)
                for j in range(2):
                    for half in range(2):
                        sp.dma_start(q_st[ROWS + half:ROWS + half + 1, s, j, :].rearrange("a (t q) -> a t q", q=P).bitcast(F32),
                                     max_rows[half * QT:(half + 1) * QT, j, :].bitcast(F32)).then_inc(rows_loaded, DMA)

            def store_o(it, s, p, c):
                b, _, h = where(it, s)
                sp.wait_ge(o_copied, p * CPB + c + 3)
                for j in range(2):
                    for dst, r in ((att_o, 0), (att_l, HD)):
                        sp.dma_start(dst[ds(b, 1), ds(h + j, 1), :, c * CH:(c + 1) * CH].rearrange("b h d t -> (b h d) t"),
                                     o_sb[2 * HD * j + r:2 * HD * j + r + HD, c % 2, :]).then_inc(o_stored[c % 2], DMA)

            sp.dma_start(ident[:, :], identity).then_inc(ident_in, DMA)
            for i in range(2):
                sp.sem_inc(o_stored[i], 4 * DMA)
            load_kv(0, 0)
            for c in range(CPB):
                load_q(0, 0, c)
            for c in range(CPB - 1):
                load_q(0, 1, c)
            load_rows(0, 0, 0)

            def stage(it, s, more):
                p = it * 2 + s
                last = isinstance(it, int)
                nxt = (it, 1) if s == 0 else (it + 1, 0)
                after = (it + 1, s)
                if more:
                    sp.wait_ge(pv_done, p * NSTEP + RING)
                    load_kv(*nxt)
                    load_q(*nxt, CPB - 1)
                for c in range(CPB):
                    if more and c == CPB - 1:
                        load_rows(*nxt, p + 1)
                    if c < CPB - 1 and not last:
                        sp.wait_ge(s_ready, p * NSTEP + CHUNK_END[c])
                        load_q(*after, c)
                    store_o(it, s, p, c)

            stages(sp, stage)
            for i in range(2):
                sp.wait_ge(o_stored[i], 4 * DMA * (NPAIR * CPB // 2 + 1))

        @block.scalar
        def _(act):
            act.sem_inc(exp_done, 2)
            act.sem_inc(o_copied, 2)

            def copy_o(p, c):
                act.wait_ge(pv_done, p * NSTEP + CHUNK_END[c] + RING)
                act.wait_ge(o_stored[c % 2], (p * 2 + c // 2 + 1) * 4 * DMA)
                act.activation(o_sb[:, c % 2, :], ps_o[:, c % 2, :], ACT.Copy).then_inc(o_copied, 1)

            def stage(it, s, more):
                p = it * 2 + s
                for n, (c, kt) in enumerate(STEPS):
                    off = max(kt * P - c * CH, 0)
                    act.wait_ge(s_ready, p * NSTEP + n + 1)
                    act.wait_ge(pv_done, p * NSTEP + n + 1)
                    act.activation(probs[:, n % RING, :, off:CH], ps_s[:, n % 2, :, off:CH], ACT.Exp,
                                   scale=HD ** -0.5).then_inc(exp_done, 1)
                    if c and kt == 0:
                        copy_o(p, c - 1)
                copy_o(p, CPB - 1)

            stages(act, stage)

        @block.gpsimd
        def _(pool):
            def stage(it, s, more):
                p = it * 2 + s
                for n, (c, kt) in enumerate(STEPS):
                    off = kt * P - c * CH
                    if off >= 0:
                        wait_apart(pool, exp_done, p * NSTEP + n + 3, pool_passed)
                        diagonal = probs[:, n % RING, :, off:off + P]
                        pool.affine_select(out=diagonal, in_=diagonal, compare_op=ALU.is_ge, fill=0.0, base=0,
                                           pattern=[[0, 2], [1, P]], channel_multiplier=-1).then_inc(masked, 1)

            pool.memset(causal[:, :], 0.0).then_inc(causal_ready, 1)
            pool.wait_ge(causal_ready, 1)
            pool.affine_select(out=causal[:, CH - P:CH], in_=causal[:, CH - P:CH], compare_op=ALU.is_ge, fill=LOWEST,
                               base=0, pattern=[[-1, P]], channel_multiplier=1).then_inc(causal_ready, 1)
            stages(pool, stage)

        @block.vector
        def _(dve):
            dve.sem_inc(m_used, 2)
            dve.memset(part_max[:, :, :, :], LOWEST)
            dve.memset(k_st[ROWS:ROWS + 2, :, :].bitcast(F32), 1.0)
            dve.memset(v_st[:, :, :, HD:2 * HD], 1.0).then_inc(ones_ready, 1)
            dve.wait_ge(ones_ready, 1)
            dve.wait_ge(causal_ready, 2)

            def unit(p, n):
                if n < len(UNITS):
                    j, t, g = UNITS[n]
                    w = min(CH, (t + 1) * P - g * CH)
                    if g == t * P // CH:
                        wait_apart(dve, m_ready, p * NUNIT + n + 1, dve_passed)
                        dve.tensor_tensor_reduce(scratch[:, n % 2, 0:w], ps_m[:, n % 2, 0:w], causal[:, CH - w:CH], 1.0, LOWEST,
                                                 ALU.add, ALU.max, part_max[:, j, t, g:g + 1]).then_inc(m_used, 1)
                    else:
                        dve.wait_ge(m_ready, p * NUNIT + n + 1)
                        dve.tensor_reduce(part_max[:, j, t, g:g + 1], ps_m[:, n % 2, 0:w], AX.X, ALU.max).then_inc(m_used, 1)
                else:
                    dve.wait_ge(m_ready, p * NUNIT + n + 1)
                    dve.tensor_copy(max_rows[:, n % 2, :], ps_m[0:2 * QT, n % 2, 0:P]).then_inc(m_used, 1)

            def finish(p):
                dve.wait_ge(m_used, p * NUNIT + len(UNITS) + 2)
                dve.tensor_reduce(neg_max[:, :, :], part_max[:, :, :, :], AX.X, ALU.max, negate=True).then_inc(max_step, 1)
                dve.wait_ge(max_step, p * 3 + 1)
                dve.tensor_copy(max_halves[:, :, 0, :], neg_max[:, :, :]).then_inc(max_step, 1)
                dve.wait_ge(max_step, p * 3 + 2)
                dve.tensor_tensor(max_halves[:, :, 1, :], neg_max[:, :, :], max_halves[:, :, 0, :].bitcast(F32),
                                  ALU.subtract).then_inc(max_step, 1)

            for n in range(NUNIT):
                if n == len(UNITS):
                    finish(0)
                unit(0, n)

            def stage(it, s, more):
                p = it * 2 + s
                if more:
                    for units in slots_of_units:
                        for n in units:
                            if n == len(UNITS):
                                finish(p + 1)
                            unit(p + 1, n)

            stages(dve, stage)

        @block.tensor
        def _(pe):
            def unit(p, s, n):
                pe.wait_ge(m_used, p * NUNIT + n + 1)
                if n < len(UNITS):
                    j, t, g = UNITS[n]
                    w = min(CH, (t + 1) * P - g * CH)
                    pe.matmul(ps_m[:, n % 2, 0:w], q_st[0:ROWS, s, j, t * P:(t + 1) * P],
                              k_st[0:ROWS, s, g * CH:g * CH + w], start=True, stop=True).then_inc(m_ready, 1)
                else:
                    j = n - len(UNITS)
                    pe.wait_ge(max_step, p * 3 + 3)
                    pe.transpose(ps_m[0:2 * QT, n % 2, 0:P], max_halves[:, j, :, :].bitcast(F32), ident[:, :]).then_inc(m_ready, 1)

            def loads(it, s, c):
                pe.wait_ge(kv_loaded[s], (it * 3 + 3) * DMA)
                pe.wait_ge(q_loaded[s], (it + 1) * 4 * CPB * DMA)

            pe.sem_inc(pv_done, RING)
            pe.wait_ge(ident_in, DMA)
            pe.wait_ge(ones_ready, 1)
            loads(0, 0, 0)
            for n in range(NUNIT):
                unit(0, 0, n)

            def stage(it, s, more):
                p = it * 2 + s
                pe.wait_ge(rows_loaded, (p + 1) * 4 * DMA)

                def pv(n):
                    c, kt = STEPS[n]
                    off = max(kt * P - c * CH, 0)
                    if kt == 0:
                        pe.wait_ge(o_copied, p * CPB + c + 1)
                    pe.wait_ge(exp_done, p * NSTEP + n + 3)
                    if kt * P >= c * CH:
                        pe.wait_ge(masked, p * NDIAG + sum(b * P >= a * CH for a, b in STEPS[:n + 1]))
                    for j in range(2):
                        ins = pe.matmul(ps_o[2 * HD * j:2 * HD * (j + 1), c % 2, off:CH], v_st[:, s, kt, :],
                                        probs[:, n % RING, j, off:CH], start=(kt == 0), stop=(n + 1 in CHUNK_END),
                                        skip_group_check=True)
                    ins.then_inc(pv_done, 1)

                for n, (c, kt) in enumerate(STEPS):
                    off = max(kt * P - c * CH, 0)
                    pe.wait_ge(exp_done, p * NSTEP + n + 1)
                    for j in range(2):
                        ins = pe.matmul(ps_s[:, n % 2, j, off:CH], k_st[0:ROWS + 2, s, kt * P:(kt + 1) * P],
                                        q_st[0:ROWS + 2, s, j, c * CH + off:(c + 1) * CH], start=True, stop=True)
                    ins.then_inc(s_ready, 1)
                    if more:
                        if n == FIRST_UNIT:
                            loads(it if s == 0 else it + 1, 1 - s, c)
                        for m in slots_of_units[n]:
                            unit(p + 1, 1 - s, m)
                    if n:
                        pv(n - 1)
                pv(NSTEP - 1)

            stages(pe, stage)


class Norm:

    def __init__(self, nc, ctx, ones, number):
        def sem(name):
            return ctx.enter_context(nc.semaphore(f"{name}_{number}"))

        self.ones = ones
        self.work = ctx.enter_context(nc.sbuf_tensor(f"norm_work_{number}", [P, KT, CH], F32))
        self.mean = ctx.enter_context(nc.sbuf_tensor(f"norm_mean_{number}", [P, CH], F32))
        self.root = ctx.enter_context(nc.sbuf_tensor(f"norm_root_{number}", [P, CH], F32))
        self.eps = ctx.enter_context(nc.sbuf_tensor(f"norm_eps_{number}", [P, 1], F32))
        self.psum = ctx.enter_context(nc.psum_tensor(f"norm_psum_{number}", [P, 2, CH], F32))
        self.z_ready = sem("z_ready")
        self.tree = sem("norm_tree")
        self.summed = sem("norm_summed")
        self.centre = sem("norm_centre")
        self.squared = sem("norm_squared")
        self.rooted = sem("norm_rooted")
        self.scaled = sem("norm_scaled")

    def pool_sum(self, pool, n, src, first):
        w = self.work
        pool.tensor_tensor(w[:, 0:4, :], src[:, 0:4, :], src[:, 4:8, :], ALU.add).then_inc(self.tree, 1)
        pool.wait_ge(self.tree, n * 6 + first + 1)
        pool.tensor_tensor(w[:, 0:2, :], w[:, 0:2, :], w[:, 2:4, :], ALU.add).then_inc(self.tree, 1)
        pool.wait_ge(self.tree, n * 6 + first + 2)
        pool.tensor_tensor(w[:, 0, :], w[:, 0, :], w[:, 1, :], ALU.add).then_inc(self.tree, 1)

    def pool(self, pool, n, z):
        pool.wait_ge(self.z_ready, n + 1)
        pool.wait_ge(self.summed, n * 2 + 1)
        self.pool_sum(pool, n, z, 0)
        pool.wait_ge(self.squared, n + 1)
        self.pool_sum(pool, n, self.work, 3)

    def pe(self, pe, n, i):
        pe.wait_ge(self.tree, n * 6 + 3 * i + 3)
        pe.matmul(self.psum[:, i, :], self.ones, self.work[:, 0, :], start=True, stop=True).then_inc(self.summed, 1)

    def dve_centre(self, dve, n, z):
        dve.wait_ge(self.summed, n * 2 + 2)
        dve.tensor_scalar(self.mean[:, :], self.psum[:, 0, :], 1.0 / D, None, ALU.mult).then_inc(self.centre, 1)
        dve.wait_ge(self.centre, n * 2 + 1)
        dve.tensor_tensor(z, z, self.mean[:, :].unsqueeze(1).to_broadcast([P, KT, CH]), ALU.subtract).then_inc(self.centre, 1)

    def act_square(self, act, n, z):
        act.wait_ge(self.centre, n * 2 + 2)
        act.activation(self.work[:, :, :], z, ACT.Square).then_inc(self.squared, 1)

    def act_root(self, act, n):
        act.wait_ge(self.summed, n * 2 + 3)
        act.wait_ge(self.scaled, n * 2 + 1)
        act.activation(self.root[:, :], self.psum[:, 1, :], ACT.Sqrt, bias=self.eps[:, :], scale=1.0 / D).then_inc(self.rooted, 1)

    def dve_scale(self, dve, n, z):
        dve.wait_ge(self.rooted, n + 1)
        dve.reciprocal(self.root[:, :], self.root[:, :]).then_inc(self.scaled, 1)
        dve.wait_ge(self.scaled, n * 2 + 2)
        dve.tensor_tensor(z, z, self.root[:, :].unsqueeze(1).to_broadcast([P, KT, CH]), ALU.mult).then_inc(self.scaled, 1)


def chunks(eng, chunk):
    chunk(0, 0, True, False)
    with eng.Fori(0, (NCH - 2) // 2) as it:
        for u in range(2):
            chunk(it * 2 + u + 1, (u + 1) % 2, False, False)
    chunk(NCH - 1, (NCH - 1) % 2, False, True)


def mix(nc, xT, att_o, att_l, woT, bias_o, x1):
    with ExitStack() as ctx:
        def sb(name, shape, dt):
            return ctx.enter_context(nc.sbuf_tensor(name, shape, dt))

        def sem(name):
            return ctx.enter_context(nc.semaphore(name))

        w_hi = sb("wo_hi", [P, KT, D], F32R)
        w_lo = sb("wo_lo", [P, KT, D], F32R)
        att = sb("att", [P, KT, CH], F32)
        row_sum = sb("row_sum", [P, KT, CH], F32)
        a_hi = sb("a_hi", [P, KT, CH], F32R)
        a_lo = sb("a_lo", [P, KT, CH], F32R)
        z = sb("z3", [P, 2, KT, CH], F32)
        bo = sb("bo", [P, KT], F32)
        ones = sb("ones3", [P, P], F32)
        ps = ctx.enter_context(nc.psum_tensor("ps3", [P, 4, CH], F32))
        norm = Norm(nc, ctx, ones[:, :], 1)
        w_in = norm.work[:, :, :].rearrange("p a c -> p (a c)").rearrange("p (s n) -> p s n", s=4)

        const_ready = sem("const_ready3")
        bias_in = sem("bias_in3")
        w_loaded = [sem(f"wo_loaded{i}") for i in range(2)]
        w_hi_done = sem("wo_hi_done")
        w_split = sem("wo_split")
        att_loaded = sem("att_loaded")
        x_loaded = [sem(f"x_loaded3_{i}") for i in range(2)]
        divided = sem("divided")
        a_hi_done = sem("a_hi_done")
        a_split = sem("a_split")
        tile_ready = sem("tile_ready3")
        tile_used = sem("tile_used3")
        stored = [sem(f"stored3_{i}") for i in range(2)]
        block = ctx.enter_context(nc.Block())

        def token(c):
            return (c // CPB, (c % CPB) * CH)

        @block.sync
        def _(sp):
            def load_att(c):
                b, tok = token(c)
                for dst, src in ((att, att_o), (row_sum, att_l)):
                    sp.dma_start(dst[:, :, :], src[ds(b, 1), :, :, ds(tok, CH)].rearrange("b (k h) d t -> (b h d) k t", k=KT)).then_inc(att_loaded, DMA)

            def load_x(c, slot):
                sp.dma_start(z[:, slot, :, :], xT[:, ds(c * CH, CH)].rearrange("(k p) t -> p k t", p=P)).then_inc(x_loaded[slot], DMA)

            def store(c, slot):
                sp.wait_ge(norm.scaled, c * 2 + 3)
                sp.dma_start(x1[ds(c, 1)].rearrange("c (k p) t -> p (c k) t", p=P), z[:, slot, :, :]).then_inc(stored[slot], DMA)

            sp.dma_start(bo[:, :], bias_o).then_inc(bias_in, DMA)
            for k in range(KT):
                if k >= 4:
                    sp.wait_ge(w_split, k - 3)
                sp.dma_start(w_in[:, k % 4, :], woT[k * P:(k + 1) * P, :]).then_inc(w_loaded[k % 2], DMA)
                if k % 2 == 1:
                    sp.wait_ge(w_loaded[0], (k // 2 + 1) * DMA)
                    sp.wait_ge(w_loaded[1], (k // 2 + 1) * DMA)
            for i in range(2):
                sp.sem_inc(stored[i], DMA)
            load_att(0)
            load_x(0, 0)

            def chunk(c, slot, first, last):
                if not last:
                    sp.wait_ge(a_split, c + 2)
                    load_att(c + 1)
                if not first:
                    store(c - 1, 1 - slot)
                if not last:
                    if not first:
                        sp.wait_ge(stored[1 - slot], ((c - 1) // 2 + 2) * DMA)
                    load_x(c + 1, 1 - slot)

            chunks(sp, chunk)
            store(NCH - 1, (NCH - 1) % 2)
            for i in range(2):
                sp.wait_ge(stored[i], (NCH // 2 + 1) * DMA)

        @block.scalar
        def _(act):
            for k in range(KT):
                act.wait_ge(w_loaded[k % 2], (k // 2 + 1) * DMA)
                act.activation(w_hi[:, k, :], w_in[:, k % 4, :], ACT.Copy).then_inc(w_hi_done, 1)

            def chunk(c, slot, first, last):
                act.wait_ge(divided, c * 2 + 2)
                act.wait_ge(tile_ready, c * KT + 1)
                act.activation(a_hi[:, :, :], att[:, :, :], ACT.Copy).then_inc(a_hi_done, 1)
                if not first:
                    norm.act_square(act, c - 1, z[:, 1 - slot, :, :])
                    norm.act_root(act, c - 1)

            chunks(act, chunk)
            norm.act_square(act, NCH - 1, z[:, (NCH - 1) % 2, :, :])
            norm.act_root(act, NCH - 1)

        @block.gpsimd
        def _(pool):
            pool.memset(ones[:, :], 1.0).then_inc(const_ready, 1)
            pool.memset(norm.eps[:, :], EPS).then_inc(const_ready, 1)
            pool.wait_ge(w_split, KT)

            def chunk(c, slot, first, last):
                if not first:
                    norm.pool(pool, c - 1, z[:, 1 - slot, :, :])

            chunks(pool, chunk)
            norm.pool(pool, NCH - 1, z[:, (NCH - 1) % 2, :, :])

        @block.vector
        def _(dve):
            dve.sem_inc(tile_used, 4)
            dve.sem_inc(a_split, 1)
            dve.sem_inc(norm.scaled, 1)
            for k in range(KT):
                dve.wait_ge(w_hi_done, k + 1)
                dve.tensor_tensor(w_lo[:, k, :], w_in[:, k % 4, :], w_hi[:, k, :].bitcast(F32), ALU.subtract).then_inc(w_split, 1)
            dve.wait_ge(bias_in, DMA)

            def divide(c):
                dve.wait_ge(att_loaded, (c + 1) * 2 * DMA)
                dve.reciprocal(row_sum[:, :, :], row_sum[:, :, :]).then_inc(divided, 1)
                dve.wait_ge(divided, c * 2 + 1)
                dve.tensor_tensor(att[:, :, :], att[:, :, :], row_sum[:, :, :], ALU.mult).then_inc(divided, 1)

            divide(0)

            def chunk(c, slot, first, last):
                dve.wait_ge(a_hi_done, c + 1)
                dve.tensor_tensor(a_lo[:, :, :], att[:, :, :], a_hi[:, :, :].bitcast(F32), ALU.subtract).then_inc(a_split, 1)
                dve.wait_ge(x_loaded[slot], (c // 2 + 1) * DMA)
                for m in range(KT):
                    dve.wait_ge(tile_ready, c * KT + m + 2)
                    ins = dve.scalar_tensor_tensor(out=z[:, slot, m, :], in0=ps[:, m % 4, :], scalar=bo[:, m:m + 1],
                                                   in1=z[:, slot, m, :], op0=ALU.add, op1=ALU.add)
                    ins.then_inc(tile_used, 1)
                    if m == 2 and not first:
                        norm.dve_centre(dve, c - 1, z[:, 1 - slot, :, :])
                    if m == 4 and not last:
                        divide(c + 1)
                    if m == 6 and not first:
                        norm.dve_scale(dve, c - 1, z[:, 1 - slot, :, :])
                dve.wait_ge(tile_used, (c + 1) * KT + 4)
                dve.sem_inc(norm.z_ready, 1)

            chunks(dve, chunk)
            norm.dve_centre(dve, NCH - 1, z[:, (NCH - 1) % 2, :, :])
            norm.dve_scale(dve, NCH - 1, z[:, (NCH - 1) % 2, :, :])

        @block.tensor
        def _(pe):
            pe.sem_inc(tile_ready, 1)
            pe.sem_inc(norm.summed, 1)
            pe.wait_ge(const_ready, 2)
            pe.wait_ge(w_split, KT)

            def chunk(c, slot, first, last):
                pe.wait_ge(a_split, c + 2)
                for m in range(KT):
                    pe.wait_ge(tile_used, c * KT + m + 1)
                    terms = [(w, a, k) for k in range(KT) for w, a in ((w_hi, a_hi), (w_hi, a_lo), (w_lo, a_hi))]
                    for i, (w, a, k) in enumerate(terms):
                        ins = pe.matmul(ps[:, m % 4, :], w[:, k, m * P:(m + 1) * P], a[:, k, :],
                                        start=(i == 0), stop=(i == len(terms) - 1))
                    ins.then_inc(tile_ready, 1)
                    if m == 2 and not first:
                        norm.pe(pe, c - 1, 0)
                    if m == 5 and not first:
                        norm.pe(pe, c - 1, 1)

            chunks(pe, chunk)
            norm.pe(pe, NCH - 1, 0)
            norm.pe(pe, NCH - 1, 1)


def feed(nc, x1, perm, up, down, out):
    with ExitStack() as ctx:
        def sb(name, shape, dt):
            return ctx.enter_context(nc.sbuf_tensor(name, shape, dt))

        def sem(name):
            return ctx.enter_context(nc.semaphore(name))

        MT = FM // P
        t_in = sb("t_in", [P, FH, CH], F32)
        t_st = sb("t_st", [P, FH, CH], F32R)
        up_hi = sb("up_hi", [P, FH, FM], F32R)
        up_lo = sb("up_lo", [P, FH, FM], F32R)
        w_dn = sb("w_dn", [P, FH, MT, FD], F32)
        act_out = sb("act_out", [P, 4, MT, CH], F32)
        z = sb("z4", [P, 2, KT, CH], F32)
        index = sb("index", [P, FH + KT], I32)
        gather_rows = sb("gather_rows", [P, FH], I32)
        scatter_rows = sb("scatter_rows", [P, KT], I32)
        ones = sb("ones4", [P, P], F32)
        ps_u = ctx.enter_context(nc.psum_tensor("ps_u", [P, 2, MT, CH], F32))
        ps_d = ctx.enter_context(nc.psum_tensor("ps_d", [P, 2, CH], F32))
        norm = Norm(nc, ctx, ones[:, :], 2)
        up_in = t_in[:, 0:FH // 2, :].rearrange("p h c -> p (h c)").rearrange("p (h m) -> p h m", h=FH)

        const_ready = sem("const_ready4")
        index_in = sem("index_in")
        w_loaded = sem("w_loaded4")
        up_hi_done = sem("up_hi_done")
        up_split = sem("up_split")
        rows_ready = sem("rows_ready")
        scatter_ready = sem("scatter_ready")
        gathered = sem("gathered")
        t_hi_done = sem("t_hi_done")
        t_split = sem("t_split")
        up_ready = sem("up_ready")
        gelu_done = sem("gelu_done")
        down_ready = sem("down_ready")
        z_added = sem("z_added")
        stored = [sem(f"stored4_{i}") for i in range(2)]
        scattered = sem("scattered")
        passed = sem("passed4")
        block = ctx.enter_context(nc.Block())
        x1_rows = x1.rearrange("c d t -> (c d) t")
        out_rows = out.rearrange("c d t -> (c d) t")
        NP2 = FH // 2

        @block.sync
        def _(sp):
            sp.dma_start(index[:, :], perm).then_inc(index_in, DMA)
            for half in range(2):
                sp.dma_start(up_in[half * FD:(half + 1) * FD], up.rearrange("h d m -> d h m")).then_inc(w_loaded, DMA)
            sp.dma_start(w_dn[:, :, :, :], down.rearrange("h (m p) d -> p h m d", p=P)).then_inc(w_loaded, DMA)

        @block.scalar
        def _(act):
            act.sem_inc(gelu_done, 2)
            act.wait_ge(w_loaded, 3 * DMA)
            act.activation(up_hi[:, :, :], up_in, ACT.Copy).then_inc(up_hi_done, 1)

            def chunk(c, slot, first, last):
                act.wait_ge(gathered, (c + 1) * FH * DMA)
                act.wait_ge(up_ready, c * FH + 1)
                act.activation(t_st[:, :, :], t_in[:, :, :], ACT.Copy).then_inc(t_hi_done, 1)
                for h in range(FH):
                    act.wait_ge(up_ready, c * FH + h + 2)
                    act.wait_ge(down_ready, c * NP2 + h // 2 + 1)
                    act.activation(act_out[:, h % 4, :, :], ps_u[:, h % 2, :, :], ACT.Gelu).then_inc(gelu_done, 1)
                    if h == 7 and not first:
                        norm.act_square(act, c - 1, z[:, 1 - slot, :, :])
                    if h == 13 and not first:
                        norm.act_root(act, c - 1)

            chunks(act, chunk)
            norm.act_square(act, NCH - 1, z[:, (NCH - 1) % 2, :, :])
            norm.act_root(act, NCH - 1)

        @block.gpsimd
        def _(pool):
            pool.memset(ones[:, :], 1.0).then_inc(const_ready, 1)
            pool.memset(norm.eps[:, :], EPS).then_inc(const_ready, 1)
            pool.sem_inc(scattered, 2)
            pool.wait_ge(index_in, DMA)
            pool.tensor_copy(gather_rows[:, :], index[:, 0:FH]).then_inc(rows_ready, 1)
            pool.tensor_copy(scatter_rows[:, :], index[:, FH:FH + KT]).then_inc(scatter_ready, 1)
            pool.wait_ge(up_split, 1)

            def gather(c):
                wait_apart(pool, rows_ready, c + 1, passed)
                for h in range(FH):
                    pool.indirect_dma_start(t_in[:, h, :], None, x1_rows,
                                            bass.IndirectOffsetOnAxis(ap=gather_rows[:, h:h + 1].bitcast(U32), axis=0)).then_inc(gathered, DMA)

            def scatter(c, slot):
                pool.wait_ge(norm.scaled, c * 2 + 3)
                wait_apart(pool, scatter_ready, c + 1, passed)
                for k in range(KT):
                    pool.indirect_dma_start(out_rows, bass.IndirectOffsetOnAxis(ap=scatter_rows[:, k:k + 1].bitcast(U32), axis=0),
                                            z[:, slot, k, :], None).then_inc(stored[slot], DMA)

            def next_rows(rows, done):
                pool.tensor_scalar(rows, rows, float(D), None, ALU.add).then_inc(done, 1)

            gather(0)

            def chunk(c, slot, first, last):
                if not last:
                    wait_apart(pool, gathered, (c + 1) * FH * DMA, passed)
                    next_rows(gather_rows[:, :], rows_ready)
                if not first:
                    norm.pool(pool, c - 1, z[:, 1 - slot, :, :])
                if not last:
                    wait_apart(pool, z_added, (c + 1) * NP2 + 2, passed)
                    gather(c + 1)
                if not first:
                    scatter(c - 1, 1 - slot)
                    wait_apart(pool, stored[1 - slot], ((c - 1) // 2 + 1) * KT * DMA, scattered)
                    next_rows(scatter_rows[:, :], scatter_ready)

            chunks(pool, chunk)
            norm.pool(pool, NCH - 1, z[:, (NCH - 1) % 2, :, :])
            scatter(NCH - 1, (NCH - 1) % 2)
            for i in range(2):
                pool.wait_ge(stored[i], NCH // 2 * KT * DMA)

        @block.vector
        def _(dve):
            dve.sem_inc(z_added, 2)
            dve.sem_inc(norm.scaled, 1)
            dve.wait_ge(up_hi_done, 1)
            dve.tensor_tensor(up_lo[:, :, :], up_in, up_hi[:, :, :].bitcast(F32), ALU.subtract).then_inc(up_split, 1)

            def chunk(c, slot, first, last):
                dve.wait_ge(t_hi_done, c + 1)
                low = t_st[FD:P, :, :]
                dve.tensor_tensor(low, t_in[FD:P, :, :], low.bitcast(F32), ALU.subtract).then_inc(t_split, 1)
                dve.wait_ge(scattered, c + 1)
                for i in range(NP2):
                    dve.wait_ge(down_ready, c * NP2 + i + 3)
                    for half in range(2):
                        rows = slice(half * FD, (half + 1) * FD)
                        ins = dve.tensor_tensor(z[rows, slot, i, :], ps_d[rows, i % 2, :], t_in[rows, 2 * i + half, :], ALU.add)
                    ins.then_inc(z_added, 1)
                    if i == 1 and not first:
                        norm.dve_centre(dve, c - 1, z[:, 1 - slot, :, :])
                    if i == 6 and not first:
                        norm.dve_scale(dve, c - 1, z[:, 1 - slot, :, :])
                dve.wait_ge(z_added, (c + 1) * NP2 + 2)
                dve.sem_inc(norm.z_ready, 1)

            chunks(dve, chunk)
            norm.dve_centre(dve, NCH - 1, z[:, (NCH - 1) % 2, :, :])
            norm.dve_scale(dve, NCH - 1, z[:, (NCH - 1) % 2, :, :])

        @block.tensor
        def _(pe):
            pe.sem_inc(up_ready, 1)
            pe.sem_inc(down_ready, 2)
            pe.sem_inc(norm.summed, 1)
            pe.wait_ge(const_ready, 2)
            pe.wait_ge(w_loaded, 3 * DMA)
            pe.wait_ge(up_split, 1)

            def chunk(c, slot, first, last):
                pe.wait_ge(t_split, c + 1)

                def down_pair(i):
                    pe.wait_ge(gelu_done, c * FH + 2 * i + 4)
                    pe.wait_ge(z_added, c * NP2 + i + 1)
                    for m in range(MT):
                        for half in range(2):
                            h = 2 * i + half
                            ins = pe.matmul(ps_d[half * FD:(half + 1) * FD, i % 2, :], w_dn[:, h, m, :], act_out[:, h % 4, m, :],
                                            start=(m == 0), stop=(m == MT - 1), skip_group_check=True)
                    ins.then_inc(down_ready, 1)

                for h in range(FH):
                    pe.wait_ge(gelu_done, c * FH + h + 1)
                    for m in range(MT):
                        for i, w in enumerate((up_hi, up_lo)):
                            ins = pe.matmul(ps_u[:, h % 2, m, :], w[:, h, m * P:(m + 1) * P], t_st[:, h, :], start=(i == 0), stop=(i == 1))
                    ins.then_inc(up_ready, 1)
                    if h % 2 == 0 and h:
                        down_pair(h // 2 - 1)
                    if h == 3 and not first:
                        norm.pe(pe, c - 1, 0)
                    if h == 12 and not first:
                        norm.pe(pe, c - 1, 1)
                down_pair(NP2 - 1)

            chunks(pe, chunk)
            norm.pe(pe, NCH - 1, 0)
            norm.pe(pe, NCH - 1, 1)


def build(nc, arrays, phases=4):
    def given(name):
        a = arrays[name]
        return nc.dram_tensor(name, a.shape, mybir.dt.from_np(a.dtype), kind="ExternalInput").ap()

    def kept(name, shape):
        return nc.dram_tensor(name, shape, F32, kind="Internal").ap()

    g = {name: given(name) for name in arrays}
    out = nc.dram_tensor("out_0_dram", [NCH, D, CH], F32, kind="ExternalOutput").ap()
    qk_halves = kept("qk_halves", [B, H + KV, 4, HALF, S])
    v_keys = kept("v_keys", [B, KV, P, S // P, HD])
    att_o = kept("att_o", [B, H, HD, S])
    att_l = kept("att_l", [B, H, HD, S])
    x1 = kept("x1", [NCH, D, CH])
    project(nc, g["xT"], g["wqkvT"], g["bias_qk"], g["bias_v"], g["cos"], g["sin"], qk_halves, v_keys)
    if phases >= 2:
        attend(nc, qk_halves, v_keys, g["identity"], att_o, att_l)
    if phases >= 3:
        mix(nc, g["xT"], att_o, att_l, g["woT"], g["bias_o"], x1)
    if phases >= 4:
        feed(nc, x1, g["perm"], g["up"], g["down"], out)


def host_layout(L0_attn_x, L0_attn_w_qkv, L0_attn_b_qkv, L0_attn_w_o, L0_attn_b_o, L0_ffn_up, L0_ffn_down, L0_ffn_perm):
    c = np.ascontiguousarray
    rows = np.arange((H + KV) * HD).reshape(QK_PAIRS, HPT, HALF, 2).transpose(0, 3, 1, 2).reshape(-1)
    perm = np.asarray(L0_ffn_perm)
    order = np.concatenate([rows, np.arange((H + KV) * HD, (H + 2 * KV) * HD)])
    inv_freq = np.float32(1.0) / np.power(np.float32(10000.0), np.arange(0, HD, 2, dtype=np.float32) / np.float32(HD))
    angle = np.arange(S, dtype=np.float32)[None, :] * inv_freq[:, None]
    return {
        "xT": c(np.asarray(L0_attn_x).reshape(T, D).T),
        "wqkvT": c(np.asarray(L0_attn_w_qkv)[order].T),
        "bias_qk": c(np.asarray(L0_attn_b_qkv)[rows].reshape(2 * QK_PAIRS, P).T),
        "bias_v": c(np.asarray(L0_attn_b_qkv)[(H + KV) * HD:]),
        "woT": c(np.asarray(L0_attn_w_o).T),
        "bias_o": c(np.asarray(L0_attn_b_o).reshape(KT, P).T),
        "up": c(np.asarray(L0_ffn_up)),
        "down": c(np.asarray(L0_ffn_down)),
        "perm": c(np.concatenate([np.tile(perm.reshape(FH, FD).T, (2, 1)), perm.reshape(KT, P).T], axis=1)),
        "cos": c(np.tile(np.cos(angle.astype(np.float64)).astype(np.float32), (HPT, 1))),
        "sin": c(np.tile(np.sin(angle.astype(np.float64)).astype(np.float32), (HPT, 1))),
        "identity": np.eye(P, dtype=np.float32),
    }


def result(chunks):
    return np.ascontiguousarray(chunks.transpose(0, 2, 1).reshape(B, S, D))


def kernel(**inputs):
    import concourse.bacc as bacc
    from concourse.bass_utils import run_bass_kernel_spmd

    arrays = host_layout(**{name: np.asarray(a) for name, a in inputs.items()})
    nc = bacc.Bacc("TRN2", target_bir_lowering=False, num_devices=1)
    build(nc, arrays)
    r = run_bass_kernel_spmd(nc, [arrays], core_ids=[0])
    return result(r.results[0]["out_0_dram"])
```

```python
from contextlib import ExitStack

import concourse.bass as bass
import numpy as np
from concourse import mybir
from concourse.alu_op_type import AluOpType as ALU

F32 = mybir.dt.float32
F32R = mybir.dt.float32r
I32 = mybir.dt.int32
U32 = mybir.dt.uint32
ACT = mybir.ActivationFunctionType
AX = mybir.AxisListType

P = 128
B, S, D = 2, 2048, 1024
T = B * S
H, KV, HD = 32, 8, 32
HALF = HD // 2
CH = 512
NCH = T // CH
CPB = S // CH
KT = D // P
NKV = KV * HD
QK_PAIRS = (H + KV) * HALF // P
HPT = P // HALF
EPS = 1e-5
LOWEST = -3.0e38
FH, FD, FM = 16, 64, 256
DMA = 16


def ds(start, size):
    return bass.ds(start, size)


def wait_apart(eng, sem, value, passed):
    eng.wait_ge(sem, value)
    eng.sem_inc(passed, 1)


def project(nc, x_chunks, wqkvT, bias_qk, bias_v, cos, sin, qk_halves, v_keys):
    with ExitStack() as ctx:
        def sb(name, shape, dt):
            return ctx.enter_context(nc.sbuf_tensor(name, shape, dt))

        def sem(name):
            return ctx.enter_context(nc.semaphore(name))

        NW = 2 * QK_PAIRS * P + NKV
        w_hi = sb("w_hi", [P, KT, NW], F32R)
        w_lo = sb("w_lo", [P, KT, NW], F32R)
        x_in = sb("x_in", [P, KT, CH], F32)
        w_in = x_in[:, 0:6, :].rearrange("p a c -> p (a c)").rearrange("p (s n) -> p s n", s=2)
        x_hi = sb("x_hi", [P, 2, KT, CH], F32R)
        x_lo = sb("x_lo", [P, 2, KT, CH], F32R)
        trig = sb("trig", [P, 2, CH], F32)
        prod = sb("prod", [P, 4, CH], F32)
        rot = prod[:, 0:2, :]
        halves = sb("halves", [P, 4, CH], F32R)
        v_out = sb("v_out", [P, 2, NKV], F32)
        bqk = sb("bqk", [P, 2 * QK_PAIRS], F32)
        bv = sb("bv", [P, NKV], F32)
        ps_qk = ctx.enter_context(nc.psum_tensor("ps_qk", [P, 2, 2, CH], F32))
        ps_v = ctx.enter_context(nc.psum_tensor("ps_v", [P, 2, CH], F32))

        bias_in = sem("bias_in")
        w_loaded = [sem(f"w_loaded{i}") for i in range(2)]
        w_hi_done = sem("w_hi_done")
        w_split = sem("w_split")
        x_loaded = sem("x_loaded")
        x_hi_done = sem("x_hi_done")
        x_split = sem("x_split")
        trig_loaded = sem("trig_loaded")
        qk_ready = sem("qk_ready")
        rope_mul = sem("rope_mul")
        rope_sum = sem("rope_sum")
        rope_hi = sem("rope_hi")
        rope_lo = sem("rope_lo")
        qk_stored = sem("qk_stored")
        v_ready = sem("v_ready")
        v_added = sem("v_added")
        v_stored = [sem(f"v_stored{i}") for i in range(2)]
        block = ctx.enter_context(nc.Block())
        ITER = NCH // 2

        @block.sync
        def _(sp):
            sp.dma_start(bqk[:, :], bias_qk).then_inc(bias_in, DMA)
            sp.dma_start(bv[:, :], bias_v.rearrange("(a n) -> a n", a=1).to_broadcast([P, NKV])).then_inc(bias_in, DMA)
            for k in range(KT):
                if k >= 2:
                    sp.wait_ge(w_split, k - 1)
                sp.dma_start(w_in[:, k % 2, :], wqkvT[k * P:(k + 1) * P, :]).then_inc(w_loaded[k % 2], DMA)
            sp.sem_inc(qk_stored, 4 * DMA)
            for i in range(2):
                sp.sem_inc(v_stored[i], DMA)
            sp.wait_ge(x_split, 1)
            sp.dma_start(x_in[:, :, :], x_chunks[0].rearrange("(k p) t -> p k t", p=P)).then_inc(x_loaded, DMA)
            with sp.Fori(0, ITER) as it:
                for u in range(2):
                    c = it * 2 + u
                    tok = (c % CPB) * CH
                    sp.wait_ge(rope_mul, c * QK_PAIRS + 2)
                    sp.dma_start(trig[:, 0, :], cos[:, ds(tok, CH)]).then_inc(trig_loaded, DMA)
                    sp.dma_start(trig[:, 1, :], sin[:, ds(tok, CH)]).then_inc(trig_loaded, DMA)
                    sp.wait_ge(x_split, c + 2)
                    sp.dma_start(x_in[:, :, :], x_chunks[ds((c + 1) % NCH, 1)]
                                 .rearrange("c (k p) t -> p (c k) t", p=P)).then_inc(x_loaded, DMA)
                    for j in range(QK_PAIRS):
                        sp.wait_ge(rope_lo, c * QK_PAIRS + j + 2)
                        for v in range(4):
                            sp.dma_start(qk_halves[ds(c // CPB, 1), j * HPT:(j + 1) * HPT, v, :, ds(tok, CH)]
                                         .rearrange("b h i t -> (b h) i t"),
                                         halves[:, v, :].bitcast(F32)).then_inc(qk_stored, DMA)
                    for t in range(CH // P):
                        sp.wait_ge(v_added, c * 4 + t + 5)
                        sp.dma_start(v_keys[ds(c // CPB, 1), :, :, ds((c % CPB) * 4 + t, 1), :]
                                     .rearrange("b g p k d -> p (b g) (k d)"),
                                     v_out[:, t % 2, :].rearrange("p (g d) -> p g d", d=HD)).then_inc(v_stored[t % 2], DMA)
            sp.wait_ge(qk_stored, 4 * DMA * (NCH * QK_PAIRS + 1))
            for i in range(2):
                sp.wait_ge(v_stored[i], DMA * (NCH * 2 + 1))
            sp.wait_ge(x_loaded, DMA * (NCH + 1))

        @block.scalar
        def _(act):
            for k in range(KT):
                act.wait_ge(w_loaded[k % 2], DMA * (k // 2 + 1))
                act.activation(w_hi[:, k, :], w_in[:, k % 2, :], ACT.Copy).then_inc(w_hi_done, 1)

            def split_x(c, u):
                act.wait_ge(x_loaded, (c + 1) * DMA)
                act.wait_ge(v_ready, c * 2)
                act.activation(x_hi[:, u, :, :], x_in[:, :, :], ACT.Copy).then_inc(x_hi_done, 1)

            act.wait_ge(x_loaded, DMA)
            act.activation(x_hi[:, 0, :, :], x_in[:, :, :], ACT.Copy).then_inc(x_hi_done, 1)
            with act.Fori(0, ITER) as it:
                for u in range(2):
                    c = it * 2 + u
                    for j in range(QK_PAIRS):
                        n = c * QK_PAIRS + j
                        if j == 2:
                            split_x(c + 1, 1 - u)
                        act.wait_ge(rope_sum, 2 * n + 2)
                        act.wait_ge(qk_stored, (n + 1) * 4 * DMA)
                        act.activation(halves[:, 0:2, :], rot, ACT.Copy).then_inc(rope_hi, 1)

        @block.gpsimd
        def _(pool):
            pool.sem_inc(rope_lo, 1)
            with pool.Fori(0, ITER) as it:
                for u in range(2):
                    for j in range(QK_PAIRS):
                        n = (it * 2 + u) * QK_PAIRS + j
                        pool.wait_ge(rope_mul, n + 3)
                        pool.tensor_tensor(prod[:, 0, :], prod[:, 0, :], prod[:, 2, :], ALU.subtract).then_inc(rope_sum, 1)
                        pool.tensor_tensor(prod[:, 1, :], prod[:, 1, :], prod[:, 3, :], ALU.add).then_inc(rope_sum, 1)
                        pool.wait_ge(rope_hi, n + 1)
                        pool.tensor_tensor(halves[:, 2:4, :], rot, halves[:, 0:2, :].bitcast(F32), ALU.subtract).then_inc(rope_lo, 1)

        @block.vector
        def _(dve):
            dve.sem_inc(rope_mul, 2)
            dve.sem_inc(v_added, 4)
            for k in range(KT):
                dve.wait_ge(w_hi_done, k + 1)
                ins = dve.tensor_tensor(w_lo[:, k, :], w_in[:, k % 2, :], w_hi[:, k, :].bitcast(F32), ALU.subtract)
                ins.then_inc(w_split, 1)
            dve.wait_ge(w_split, KT)
            dve.sem_inc(x_split, 1)
            dve.wait_ge(bias_in, 2 * DMA)

            def split_x(c, u):
                dve.wait_ge(x_hi_done, c + 1)
                dve.tensor_tensor(x_lo[:, u, :, :], x_in[:, :, :], x_hi[:, u, :, :].bitcast(F32), ALU.subtract).then_inc(x_split, 1)

            dve.wait_ge(x_hi_done, 1)
            dve.tensor_tensor(x_lo[:, 0, :, :], x_in[:, :, :], x_hi[:, 0, :, :].bitcast(F32), ALU.subtract).then_inc(x_split, 1)
            with dve.Fori(0, ITER) as it:
                for u in range(2):
                    c = it * 2 + u
                    for j in range(QK_PAIRS):
                        n = c * QK_PAIRS + j
                        if j == 3:
                            split_x(c + 1, 1 - u)
                        if j == 0:
                            dve.wait_ge(trig_loaded, (c + 1) * 2 * DMA)
                        dve.wait_ge(qk_ready, n + 1)
                        dve.wait_ge(rope_lo, n + 1)
                        for k, (part, table) in enumerate(((0, 0), (1, 0), (1, 1), (0, 1))):
                            ins = dve.scalar_tensor_tensor(
                                out=prod[:, k, :], in0=ps_qk[:, j % 2 if u == 0 else (j + QK_PAIRS) % 2, part, :],
                                scalar=bqk[:, 2 * j + part:2 * j + part + 1], in1=trig[:, table, :],
                                op0=ALU.add, op1=ALU.mult)
                        ins.then_inc(rope_mul, 1)
                    for t in range(CH // P):
                        if t % 2 == 0:
                            dve.wait_ge(v_ready, c * 2 + t // 2 + 3)
                        dve.wait_ge(v_stored[t % 2], (c * 2 + t // 2 + 1) * DMA)
                        dve.tensor_tensor(v_out[:, t % 2, :], ps_v[:, t // 2, (t % 2) * NKV:(t % 2 + 1) * NKV],
                                          bv[:, :], ALU.add).then_inc(v_added, 1)

        @block.tensor
        def _(pe):
            pe.sem_inc(v_ready, 2)
            pe.wait_ge(w_split, KT)
            with pe.Fori(0, ITER) as it:
                for u in range(2):
                    c = it * 2 + u
                    pe.wait_ge(x_split, c + 2)
                    for j in range(QK_PAIRS):
                        n = c * QK_PAIRS + j
                        pe.wait_ge(rope_mul, n + 1)
                        for part in range(2):
                            cols = slice((2 * j + part) * P, (2 * j + part + 1) * P)
                            terms = [(w, x, k) for k in range(KT) for w, x in ((w_hi, x_hi), (w_hi, x_lo), (w_lo, x_hi))]
                            for i, (w, x, k) in enumerate(terms):
                                ins = pe.matmul(ps_qk[:, j % 2 if u == 0 else (j + QK_PAIRS) % 2, part, :], w[:, k, cols], x[:, u, k, :],
                                                start=(i == 0), stop=(i == len(terms) - 1))
                        ins.then_inc(qk_ready, 1)
                    for t in range(CH // P):
                        if t % 2 == 0:
                            pe.wait_ge(v_added, c * 4 + t + 2)
                        cols = slice(2 * QK_PAIRS * P, NW)
                        terms = [(w, x, k) for k in range(KT) for w, x in ((w_hi, x_hi), (w_lo, x_hi), (w_hi, x_lo))]
                        for i, (w, x, k) in enumerate(terms):
                            ins = pe.matmul(ps_v[:, t // 2, (t % 2) * NKV:(t % 2 + 1) * NKV],
                                            x[:, u, k, t * P:(t + 1) * P], w[:, k, cols],
                                            start=(i == 0), stop=(i == len(terms) - 1))
                        if t % 2 == 1:
                            ins.then_inc(v_ready, 1)


QT = S // P
SLOTS = 2
NPAIR = B * H // 2
STEPS = [(c, kt) for c in range(CPB) for kt in range((c + 1) * CH // P)]
NSTEP = len(STEPS)
CHUNK_END = [STEPS.index((c, (c + 1) * CH // P - 1)) + 1 for c in range(CPB)]
ROWS = 3 * HD
RING = 4
OB, MB = 1, 3
TPC = CH // P
ROWS_AFTER = 3
LEAD = 17
LAG = 2


def units_of_maxima():
    units = []
    for c in range(CPB):
        mine = [(j, t, g) for t in range(c * TPC, (c + 1) * TPC) for g in range(c + 1) for j in range(2)]
        if c:
            mine.insert(ROWS_AFTER, ("rows", c - 1))
        units += mine
    return units + [("rows", CPB - 1)]


UNITS = units_of_maxima()
NUNIT = len(UNITS)
assert NUNIT % MB == 0


def units_before(step):
    width = [CH - max(kt * P - c * CH, 0) for c, kt in STEPS]
    width = width[LEAD:] + width[:LEAD]
    return NUNIT if step == NSTEP else (NUNIT - 1) * sum(width[:step]) // sum(width[:-1])


EARLY = units_before(NSTEP - LEAD)


def units_at(step):
    own = range(units_before(NSTEP - LEAD + step), units_before(NSTEP - LEAD + step + 1)) if step < LEAD else ()
    nxt = range(units_before(step - LEAD), units_before(step - LEAD + 1)) if step >= LEAD else ()
    return own, nxt


BETWEEN = {0: (0, 0, 0, 0), 1: (0,0,0,1), 2: (0,1,0,1), 3: (1,1,0,1), 4: (1, 1, 1, 1)}


EARLY_ROWS = [c for c in range(CPB) if UNITS.index(("rows", c)) < EARLY]


def attend(nc, qk_halves, v_keys, identity, w_o, perm, wo_hi, wo_lo, att_o, att_l):
    with ExitStack() as ctx:
        def sb(name, shape, dt):
            return ctx.enter_context(nc.sbuf_tensor(name, shape, dt))

        def sem(name):
            return ctx.enter_context(nc.semaphore(name))

        q_st = sb("q_st", [P, SLOTS, 2, S], F32R)
        k_st = sb("k_st", [P, SLOTS, S], F32R)
        v_st = sb("v_st", [P, SLOTS, QT, 2 * HD], F32)
        probs = sb("probs", [P, RING, 2, CH], F32)
        o_sb = sb("o_sb", [P, 2, CH], F32)
        ident = sb("ident", [P, P], F32)
        causal = sb("causal", [P, CH], F32)
        scratch = sb("scratch", [P, MB, CH], F32)
        part_max = sb("part_max", [P, 2, QT, CPB], F32)
        neg_max = sb("neg_max", [P, 2, TPC], F32)
        max_halves = sb("max_halves", [P, 2, 2, TPC], F32R)
        max_rows = sb("max_rows", [2 * 2 * TPC, P], F32R)
        wo_rows = sb("wo_rows", [P, KT], I32)
        wo_in = sb("wo_in", [P, KT, D], F32)
        ps_s = ctx.enter_context(nc.psum_tensor("ps_s", [P, 2, 2, CH], F32))
        ps_o = ctx.enter_context(nc.psum_tensor("ps_o", [P, OB, CH], F32))
        ps_m = ctx.enter_context(nc.psum_tensor("ps_m", [P, MB, CH], F32))

        causal_ready = sem("causal_ready")
        ones_ready = sem("ones_ready")
        ident_in = sem("ident_in")
        loaded = [sem(f"loaded{i}") for i in range(SLOTS)]
        s_ready = sem("s_ready")
        exp_done = sem("exp_done")
        masked = sem("masked")
        pv_done = sem("pv_done")
        o_copied = sem("o_copied")
        o_stored = [sem(f"o_stored{i}") for i in range(2)]
        m_ready = sem("m_ready")
        m_used = sem("m_used")
        max_step = sem("max_step")
        rows_loaded = sem("rows_loaded")
        dve_passed = sem("dve_passed")
        pool_passed = sem("pool_passed")
        block = ctx.enter_context(nc.Block())
        wo_index_in = sem("wo_index_in")
        wo_gathered = sem("wo_gathered")
        wo_turned = sem("wo_turned")
        wo_hi_done = sem("wo_hi_done")
        wo_split = sem("wo_split")
        WO_BANKS = [(k, m) for k in range(KT) for m in range(0, D, CH)]
        NDIAG = CPB * TPC
        LOADS = 7
        ROW_LOADS = 4

        def stages(eng, stage):
            with eng.Fori(0, NPAIR // 2 - 1) as it:
                for s in range(SLOTS):
                    stage(it, s, True)
            stage(NPAIR // 2 - 1, 0, True)
            stage(NPAIR // 2 - 1, 1, False)

        @block.sync
        def _(sp):
            def where(it, s):
                return it // KV, it % KV, (it % KV) * 4 + 2 * s

            def load(it, s):
                b, g, h = where(it, s)
                head = qk_halves[ds(b, 1), ds(g + H, 1)].rearrange("b h v i t -> (b h v i) t")
                sp.dma_start(k_st[0:2 * HD, s, :].bitcast(F32), head).then_inc(loaded[s], DMA)
                sp.dma_start(k_st[2 * HD:3 * HD, s, :].bitcast(F32), head[0:HD, :]).then_inc(loaded[s], DMA)
                for j in range(2):
                    head = qk_halves[ds(b, 1), ds(h + j, 1)].rearrange("b h v i t -> (b h v i) t")
                    sp.dma_start(q_st[0:HD, s, j, :].bitcast(F32), head[0:HD, :]).then_inc(loaded[s], DMA)
                    sp.dma_start(q_st[HD:3 * HD, s, j, :].bitcast(F32), head).then_inc(loaded[s], DMA)
                sp.dma_start(v_st[:, s, :, 0:HD], v_keys[ds(b, 1), ds(g, 1)].rearrange("b g p k d -> (b g p) k d")).then_inc(loaded[s], DMA)

            def load_rows(p, s, c):
                sp.wait_ge(m_used, p * NUNIT + UNITS.index(("rows", c)) + 1 + MB)
                for half in range(2):
                    for j in range(2):
                        first = (2 * half + j) * TPC
                        sp.dma_start(q_st[ROWS + half:ROWS + half + 1, s, j, c * CH:(c + 1) * CH].rearrange("a (t q) -> a t q", q=P).bitcast(F32),
                                     max_rows[first:first + TPC, :].bitcast(F32)).then_inc(rows_loaded, DMA)

            def store_o(it, s, p, c):
                b, _, h = where(it, s)
                sp.wait_ge(o_copied, p * CPB + c + 1 + OB)
                for j in range(2):
                    first = 2 * HD * j
                    sp.dma_start(att_o[ds(b, 1), ds(h + j, 1), :, c * CH:(c + 1) * CH].rearrange("b h d t -> (b h d) t"),
                                 o_sb[first:first + HD, c % 2, :]).then_inc(o_stored[c % 2], DMA)
                    sp.dma_start(att_l[ds(b, 1), ds(h + j, 1), c * CH:(c + 1) * CH].rearrange("b h t -> (b h) t"),
                                 o_sb[first + HD:first + HD + 1, c % 2, :]).then_inc(o_stored[c % 2], DMA)

            sp.dma_start(wo_rows[:, :], perm).then_inc(wo_index_in, DMA)
            sp.dma_start(ident[:, :], identity).then_inc(ident_in, DMA)
            for i in range(2):
                sp.sem_inc(o_stored[i], 4 * DMA)
            sp.sem_inc(rows_loaded, ROW_LOADS * DMA)
            load(0, 0)
            for c in EARLY_ROWS:
                load_rows(0, 0, c)

            def stage(it, s, more):
                p = it * 2 + s
                late = [c for c in range(CPB) if c not in EARLY_ROWS]
                load_rows(p, s, late[0])
                if more:
                    sp.wait_ge(pv_done, p * NSTEP + RING)
                    load(*((it, 1) if s == 0 else (it + 1, 0)))
                store_o(it, s, p, 0)
                store_o(it, s, p, 1)
                for c in late[1:]:
                    load_rows(p, s, c)
                for c in EARLY_ROWS[:1] if more else ():
                    load_rows(p + 1, 1 - s, c)
                store_o(it, s, p, 2)
                for c in EARLY_ROWS[1:] if more else ():
                    load_rows(p + 1, 1 - s, c)
                store_o(it, s, p, 3)

            stages(sp, stage)
            for i in range(2):
                sp.wait_ge(o_stored[i], 4 * DMA * (NPAIR * CPB // 2 + 1))

        @block.scalar
        def _(act):
            act.sem_inc(exp_done, 2)
            act.sem_inc(o_copied, OB)
            for i, (k, m) in enumerate(WO_BANKS):
                act.wait_ge(wo_turned, i + 1)
                act.activation(wo_hi[:, k, m:m + CH], ps_s[:, i // 2 % 2, i % 2, :], ACT.Copy).then_inc(wo_hi_done, 1)

            def copy_o(p, c):
                act.wait_ge(pv_done, p * NSTEP + CHUNK_END[c] + RING)
                act.wait_ge(o_stored[c % 2], (p * 2 + c // 2 + 1) * 4 * DMA)
                act.activation(o_sb[:, c % 2, :], ps_o[:, c % OB, :], ACT.Copy).then_inc(o_copied, 1)

            def stage(it, s, more):
                p = it * 2 + s
                for n, (c, kt) in enumerate(STEPS):
                    off = max(kt * P - c * CH, 0)
                    act.wait_ge(s_ready, p * NSTEP + n + 1)
                    act.wait_ge(pv_done, p * NSTEP + n + 1)
                    act.activation(probs[:, n % RING, :, off:CH], ps_s[:, n % 2, :, off:CH], ACT.Exp,
                                   scale=HD ** -0.5).then_inc(exp_done, 1)
                    if c and kt == 0:
                        copy_o(p, c - 1)
                copy_o(p, CPB - 1)

            stages(act, stage)

        @block.gpsimd
        def _(pool):
            def stage(it, s, more):
                p = it * 2 + s
                for n, (c, kt) in enumerate(STEPS):
                    off = kt * P - c * CH
                    if off >= 0:
                        wait_apart(pool, exp_done, p * NSTEP + n + 3, pool_passed)
                        diagonal = probs[:, n % RING, :, off:off + P]
                        pool.affine_select(out=diagonal, in_=diagonal, compare_op=ALU.is_ge, fill=0.0, base=0,
                                           pattern=[[0, 2], [1, P]], channel_multiplier=-1).then_inc(masked, 1)

            pool.wait_ge(wo_index_in, DMA)
            for k in range(KT):
                pool.indirect_dma_start(wo_in[:, k, :], None, w_o,
                                        bass.IndirectOffsetOnAxis(ap=wo_rows[:, k:k + 1].bitcast(U32), axis=0)).then_inc(wo_gathered, DMA)
            pool.memset(causal[:, :], 0.0).then_inc(causal_ready, 1)
            pool.wait_ge(causal_ready, 1)
            pool.affine_select(out=causal[:, CH - P:CH], in_=causal[:, CH - P:CH], compare_op=ALU.is_ge, fill=LOWEST,
                               base=0, pattern=[[-1, P]], channel_multiplier=1).then_inc(causal_ready, 1)
            stages(pool, stage)

        @block.vector
        def _(dve):
            dve.sem_inc(m_used, MB)
            dve.memset(part_max[:, :, :, :], LOWEST)
            dve.memset(k_st[ROWS:ROWS + 2, :, :].bitcast(F32), 1.0)
            dve.memset(v_st[:, :, :, HD:2 * HD], 1.0).then_inc(ones_ready, 1)
            dve.wait_ge(ones_ready, 1)
            dve.wait_ge(causal_ready, 2)

            def unit(p, n):
                j, t, g = UNITS[n]
                w = min(CH, (t + 1) * P - g * CH)
                if g == t * P // CH:
                    wait_apart(dve, m_ready, p * NUNIT + n + 1, dve_passed)
                    dve.tensor_tensor_reduce(scratch[:, n % MB, 0:w], ps_m[:, n % MB, 0:w], causal[:, CH - w:CH], 1.0, LOWEST,
                                             ALU.add, ALU.max, part_max[:, j, t, g:g + 1]).then_inc(m_used, 1)
                else:
                    dve.wait_ge(m_ready, p * NUNIT + n + 1)
                    dve.tensor_reduce(part_max[:, j, t, g:g + 1], ps_m[:, n % MB, 0:w], AX.X, ALU.max).then_inc(m_used, 1)
                if n + 1 < NUNIT and (j, t, g) == (1, (c := t // TPC) * TPC + TPC - 1, c):
                    finish(p, c, n)

            def finish(p, c, n):
                done = (p * CPB + c) * 3
                dve.wait_ge(m_used, p * NUNIT + n + 1 + MB)
                dve.tensor_reduce(neg_max[:, :, :], part_max[:, :, c * TPC:(c + 1) * TPC, :], AX.X, ALU.max, negate=True).then_inc(max_step, 1)
                dve.wait_ge(max_step, done + 1)
                dve.tensor_copy(max_halves[:, 0, :, :], neg_max[:, :, :]).then_inc(max_step, 1)
                dve.wait_ge(max_step, done + 2)
                dve.tensor_tensor(max_halves[:, 1, :, :], neg_max[:, :, :], max_halves[:, 0, :, :].bitcast(F32),
                                  ALU.subtract).then_inc(max_step, 1)

            def rows(p, n):
                dve.wait_ge(rows_loaded, ROW_LOADS * DMA * (p * CPB + UNITS[n][1] + 1))
                dve.wait_ge(m_ready, p * NUNIT + n + 1)
                dve.tensor_copy(max_rows[:, :], ps_m[0:4 * TPC, n % MB, 0:P]).then_inc(m_used, 1)

            def maxima(p, ns):
                for n in ns:
                    (rows if UNITS[n][0] == "rows" else unit)(p, n)

            for i, (k, m) in enumerate(WO_BANKS):
                dve.wait_ge(wo_hi_done, i + 1)
                dve.tensor_tensor(wo_lo[:, k, m:m + CH], ps_s[:, i // 2 % 2, i % 2, :], wo_hi[:, k, m:m + CH].bitcast(F32),
                                  ALU.subtract).then_inc(wo_split, 1)
            maxima(0, range(EARLY))

            def stage(it, s, more):
                p = it * 2 + s
                for step in range(NSTEP):
                    own, nxt = units_at(step)
                    maxima(p, own)
                    if more:
                        maxima(p + 1, nxt)

            stages(dve, stage)

        @block.tensor
        def _(pe):
            def unit(p, s, n):
                pe.wait_ge(m_used, p * NUNIT + n + 1)
                if UNITS[n][0] == "rows":
                    pe.wait_ge(max_step, (p * CPB + UNITS[n][1]) * 3 + 3)
                    pe.transpose(ps_m[0:4 * TPC, n % MB, 0:P], max_halves[:, :, :, :].rearrange("p a j t -> p (a j t)").bitcast(F32),
                                 ident[:, :]).then_inc(m_ready, 1)
                else:
                    j, t, g = UNITS[n]
                    w = min(CH, (t + 1) * P - g * CH)
                    pe.matmul(ps_m[:, n % MB, 0:w], q_st[0:ROWS, s, j, t * P:(t + 1) * P],
                              k_st[0:ROWS, s, g * CH:g * CH + w], start=True, stop=True).then_inc(m_ready, 1)

            pe.sem_inc(pv_done, RING)
            pe.wait_ge(ident_in, DMA)
            pe.wait_ge(wo_gathered, KT * DMA)
            for i, (k, m) in enumerate(WO_BANKS):
                if i >= 4:
                    pe.wait_ge(wo_split, i - 3)
                for t in range(CH // P):
                    ins = pe.transpose(ps_s[:, i // 2 % 2, i % 2, t * P:(t + 1) * P], wo_in[:, m // P + t, k * P:(k + 1) * P], ident[:, :])
                ins.then_inc(wo_turned, 1)
            pe.wait_ge(wo_split, len(WO_BANKS))
            pe.wait_ge(ones_ready, 1)
            pe.wait_ge(loaded[0], LOADS * DMA)
            for n in range(EARLY):
                unit(0, 0, n)

            def stage(it, s, more):
                p = it * 2 + s

                def scores(n, j):
                    c, kt = STEPS[n]
                    off = max(kt * P - c * CH, 0)
                    if j == 0:
                        if kt == 0:
                            pe.wait_ge(rows_loaded, (p * CPB + c + 2) * ROW_LOADS * DMA)
                        pe.wait_ge(exp_done, p * NSTEP + n + 1)
                    ins = pe.matmul(ps_s[:, n % 2, j, off:CH], k_st[0:ROWS + 2, s, kt * P:(kt + 1) * P],
                                    q_st[0:ROWS + 2, s, j, c * CH + off:(c + 1) * CH], start=True, stop=True)
                    if j == 1:
                        ins.then_inc(s_ready, 1)

                def values(n, j):
                    c, kt = STEPS[n]
                    off = max(kt * P - c * CH, 0)
                    if j == 0:
                        if kt == 0:
                            pe.wait_ge(o_copied, p * CPB + c + 1)
                        pe.wait_ge(exp_done, p * NSTEP + n + 3)
                        if kt * P >= c * CH:
                            pe.wait_ge(masked, p * NDIAG + sum(b * P >= a * CH for a, b in STEPS[:n + 1]))
                    ins = pe.matmul(ps_o[2 * HD * j:2 * HD * (j + 1), c % OB, off:CH], v_st[:, s, kt, :],
                                    probs[:, n % RING, j, off:CH], start=(kt == 0), stop=(n + 1 in CHUNK_END),
                                    skip_group_check=True)
                    if j == 1:
                        ins.then_inc(pv_done, 1)

                for n in range(NSTEP + LAG):
                    units = []
                    if n < NSTEP:
                        own, nxt = units_at(n)
                        units = [(p, s, m) for m in own] + [(p + 1, 1 - s, m) for m in nxt if more]
                    if n == LEAD and more:
                        pe.wait_ge(loaded[1 - s], (it + 1 if s == 0 else it + 2) * LOADS * DMA)
                    for slot, after in enumerate(BETWEEN[min(len(units), 4)]):
                        if n < NSTEP and slot < 2:
                            scores(n, slot)
                        if n >= LAG and slot >= 2:
                            values(n - LAG, slot - 2)
                        for which in units[:after]:
                            unit(*which)
                        units = units[after:]
                    for which in units:
                        unit(*which)

            stages(pe, stage)


PIECE = 2
NPIECE = KT // PIECE


class Norm:

    def __init__(self, nc, ctx, ones, number, added, ahead):
        def sem(name):
            return ctx.enter_context(nc.semaphore(f"{name}_{number}"))

        self.ones, self.added, self.ahead = ones, added, ahead
        self.squares = ctx.enter_context(nc.sbuf_tensor(f"norm_squares_{number}", [P, KT, CH], F32))
        self.total = ctx.enter_context(nc.sbuf_tensor(f"norm_total_{number}", [P, 2, CH], F32))
        self.mean = ctx.enter_context(nc.sbuf_tensor(f"norm_mean_{number}", [P, CH], F32))
        self.root = ctx.enter_context(nc.sbuf_tensor(f"norm_root_{number}", [P, CH], F32))
        self.eps = ctx.enter_context(nc.sbuf_tensor(f"norm_eps_{number}", [P, 1], F32))
        self.psum = ctx.enter_context(nc.psum_tensor(f"norm_psum_{number}", [P, 2, CH], F32))
        self.tallied = sem("norm_tallied")
        self.summed = sem("norm_summed")
        self.centred = sem("norm_centred")
        self.squared = sem("norm_squared")
        self.rooted = sem("norm_rooted")
        self.scaled = sem("norm_scaled")

    def start_pe(self, pe):
        pe.sem_inc(self.summed, 2)

    def start_dve(self, dve):
        dve.sem_inc(self.scaled, 1)

    def add(self, pool, n, i, tile, src):
        total = self.total[:, i, :]
        before = n * 2 * (KT - 1) + i * (KT - 1) + tile - 1
        if tile == 1:
            pool.wait_ge(self.summed, 2 * n + 1 + i)
            pool.tensor_tensor(total, src[:, 0, :], src[:, 1, :], ALU.add).then_inc(self.tallied, 1)
        else:
            pool.wait_ge(self.tallied, before)
            pool.tensor_tensor(total, total, src[:, tile, :], ALU.add).then_inc(self.tallied, 1)

    def pool_z(self, pool, n, z, tiles):
        for tile in tiles:
            pool.wait_ge(self.added, n * KT + tile + 1 + self.ahead)
            self.add(pool, n, 0, tile, z)

    def pool_squares(self, pool, n):
        for tile in range(1, KT):
            pool.wait_ge(self.squared, n * NPIECE + tile // PIECE + 1)
            self.add(pool, n, 1, tile, self.squares)

    def pe(self, pe, n, i):
        pe.wait_ge(self.tallied, (n * 2 + i + 1) * (KT - 1))
        pe.matmul(self.psum[:, i, :], self.ones, self.total[:, i, :], start=True, stop=True).then_inc(self.summed, 1)

    def piece(self, z, i):
        return z[:, i * PIECE:(i + 1) * PIECE, :]

    def dve_centre(self, dve, n, z):
        dve.wait_ge(self.summed, n * 2 + 3)
        dve.tensor_scalar(self.mean[:, :], self.psum[:, 0, :], 1.0 / D, None, ALU.mult).then_inc(self.centred, 1)
        dve.wait_ge(self.centred, n * (NPIECE + 1) + 1)
        for i in range(NPIECE):
            dve.tensor_tensor(self.piece(z, i), self.piece(z, i), self.mean[:, :].unsqueeze(1).to_broadcast([P, PIECE, CH]),
                              ALU.subtract).then_inc(self.centred, 1)

    def act_square(self, act, n, z, i):
        act.wait_ge(self.centred, n * (NPIECE + 1) + i + 2)
        act.activation(self.piece(self.squares, i), self.piece(z, i), ACT.Square).then_inc(self.squared, 1)

    def act_root(self, act, n):
        act.wait_ge(self.summed, n * 2 + 4)
        act.wait_ge(self.scaled, n * (NPIECE + 1) + 1)
        act.activation(self.root[:, :], self.psum[:, 1, :], ACT.Sqrt, bias=self.eps[:, :], scale=1.0 / D).then_inc(self.rooted, 1)

    def dve_invert(self, dve, n):
        dve.wait_ge(self.rooted, n + 1)
        dve.reciprocal(self.root[:, :], self.root[:, :]).then_inc(self.scaled, 1)
        dve.wait_ge(self.scaled, n * (NPIECE + 1) + 2)

    def dve_scale(self, dve, z, i):
        dve.tensor_tensor(self.piece(z, i), self.piece(z, i), self.root[:, :].unsqueeze(1).to_broadcast([P, PIECE, CH]),
                          ALU.mult).then_inc(self.scaled, 1)

    def scaled_at(self, n, i):
        return n * (NPIECE + 1) + i + 3


def chunks(eng, chunk, slots, before, after):
    for c in range(before):
        chunk(c, c % slots, c, True)
    assert (NCH - before - after) % slots == 0
    with eng.Fori(0, (NCH - before - after) // slots) as it:
        for u in range(slots):
            chunk(it * slots + u + before, (u + before) % slots, before, True)
    for c in range(NCH - after, NCH):
        chunk(c, c % slots, before, c < NCH - 1)


ZS = 3


def mix(nc, x_chunks, att_o, att_l, att_inv, w_hi, w_lo, bias_o, perm, x1_hi, x1_lo):
    with ExitStack() as ctx:
        def sb(name, shape, dt):
            return ctx.enter_context(nc.sbuf_tensor(name, shape, dt))

        def sem(name):
            return ctx.enter_context(nc.semaphore(name))

        IR = 2
        att = sb("att", [P, KT, CH], F32)
        inv = sb("inv", [P, IR, CH], F32)
        a_hi = sb("a_hi", [P, KT, CH], F32R)
        a_lo = sb("a_lo", [P, KT, CH], F32R)
        z = sb("z3", [P, ZS, KT, CH], F32)
        x_hi = sb("x1_high", [P, KT, CH], F32R)
        bo = sb("bo", [P, KT], F32)
        rows = sb("rows3", [P, KT], I32)
        ones = sb("ones3", [P, P], F32)
        ps = ctx.enter_context(nc.psum_tensor("ps3", [P, 4, CH], F32))

        const_ready = sem("const_ready3")
        index_in = sem("index_in3")
        bias_in = sem("bias_in3")
        sums_in = sem("sums_in")
        inverted = sem("inverted")
        inverses_out = sem("inverses_out")
        att_loaded = sem("att_loaded")
        inv_loaded = [sem(f"inv_loaded{i}") for i in range(IR)]
        rows_ready = sem("rows_ready3")
        x_loaded = sem("x_loaded3")
        divided = sem("divided")
        a_hi_done = sem("a_hi_done")
        a_split = sem("a_split")
        a_used = sem("a_used")
        tile_ready = sem("tile_ready3")
        tile_used = sem("tile_used3")
        x_hi_done = sem("x1_hi_done")
        x_lo_done = sem("x1_lo_done")
        hi_stored = sem("hi_stored")
        lo_stored = sem("lo_stored")
        passed = sem("passed3")
        norm = Norm(nc, ctx, ones[:, :], 1, tile_used, 4)
        sums = norm.squares[:, 0:2, :].rearrange("p a c -> p (a c)")
        block = ctx.enter_context(nc.Block())
        flat = "b h (q t) -> (b h q) t"

        @block.sync
        def _(sp):
            def load_att(c):
                sp.dma_start(att[:, :, :], att_o[ds(c // CPB, 1), :, :, ds((c % CPB) * CH, CH)]
                             .rearrange("b (k h) d t -> (b h d) k t", k=KT)).then_inc(att_loaded, DMA)

            def load_inv(c):
                for k in range(KT):
                    sp.wait_ge(divided, c * KT + k + 1)
                    sp.dma_start(inv[:, k % IR, :], att_inv[ds(c // CPB, 1), k * P // HD:(k + 1) * P // HD, ds((c % CPB) * CH, CH)]
                                 .rearrange("b h t -> (b h) t").unsqueeze(1).to_broadcast([P // HD, HD, CH])).then_inc(inv_loaded[k % IR], DMA)

            def store(c, slot):
                sp.wait_ge(x_hi_done, (c + 1) * NPIECE)
                sp.dma_start(x1_hi[ds(c, 1)].rearrange("c (k p) t -> p (c k) t", p=P), x_hi[:, :, :].bitcast(F32)).then_inc(hi_stored, DMA)
                sp.wait_ge(lo_stored, (c + 2) * DMA)
                sp.wait_ge(x_lo_done, (c + 1) * NPIECE)
                sp.dma_start(x1_lo[ds(c, 1)].rearrange("c (k p) t -> p (c k) t", p=P), z[:, slot, :, :]).then_inc(lo_stored, DMA)

            sp.dma_start(rows[:, :], perm).then_inc(index_in, DMA)
            sp.dma_start(sums, att_l.rearrange(flat, q=2)).then_inc(sums_in, DMA)
            sp.sem_inc(hi_stored, DMA)
            sp.sem_inc(lo_stored, 2 * DMA)
            load_att(0)
            sp.wait_ge(inverted, 1)
            sp.dma_start(att_inv.rearrange(flat, q=2), sums).then_inc(inverses_out, DMA)
            sp.wait_ge(inverses_out, DMA)
            load_inv(0)

            def chunk(c, slot, past, more):
                if more:
                    sp.wait_ge(a_split, (c + 1) * KT)
                    load_att(c + 1)
                    load_inv(c + 1)
                if past:
                    store(c - 1, (slot - 1) % ZS)

            chunks(sp, chunk, ZS, 1, 1)
            store(NCH - 1, (NCH - 1) % ZS)
            sp.wait_ge(hi_stored, (NCH + 1) * DMA)
            sp.wait_ge(lo_stored, (NCH + 2) * DMA)

        @block.scalar
        def _(act):
            def split(n, z_of):
                for i in range(NPIECE):
                    if i == 0:
                        act.wait_ge(hi_stored, (n + 1) * DMA)
                    act.wait_ge(norm.scaled, norm.scaled_at(n, i))
                    act.activation(norm.piece(x_hi, i), norm.piece(z_of, i), ACT.Copy).then_inc(x_hi_done, 1)

            def chunk(c, slot, past, more):
                for k in range(KT):
                    act.wait_ge(divided, c * KT + k + 1 + IR)
                    act.wait_ge(a_used, c * KT + k + 1)
                    act.activation(a_hi[:, k, :], att[:, k, :], ACT.Copy).then_inc(a_hi_done, 1)
                if past:
                    behind = z[:, (slot - 1) % ZS, :, :]
                    for i in range(NPIECE):
                        norm.act_square(act, c - 1, behind, i)
                    norm.act_root(act, c - 1)
                    split(c - 1, behind)

            chunks(act, chunk, ZS, 1, 1)
            behind = z[:, (NCH - 1) % ZS, :, :]
            for i in range(NPIECE):
                norm.act_square(act, NCH - 1, behind, i)
            norm.act_root(act, NCH - 1)
            split(NCH - 1, behind)

        @block.gpsimd
        def _(pool):
            x_rows = x_chunks.rearrange("c d t -> (c d) t")

            def gather(c):
                wait_apart(pool, rows_ready, c + 1, passed)
                for k in range(KT):
                    pool.indirect_dma_start(z_slot(c)[:, k, :], None, x_rows,
                                            bass.IndirectOffsetOnAxis(ap=rows[:, k:k + 1].bitcast(U32), axis=0)).then_inc(x_loaded, DMA)

            slot_of = {}

            def z_slot(c):
                return z[:, slot_of["next"], :, :]

            pool.wait_ge(index_in, DMA)
            pool.sem_inc(rows_ready, 1)
            slot_of["next"] = 0
            gather(0)
            for k in range(KT):
                pool.indirect_dma_start(bo[:, k:k + 1], None, bias_o,
                                        bass.IndirectOffsetOnAxis(ap=rows[:, k:k + 1].bitcast(U32), axis=0)).then_inc(bias_in, DMA)
            pool.memset(ones[:, :], 1.0).then_inc(const_ready, 1)
            pool.memset(norm.eps[:, :], EPS).then_inc(const_ready, 1)
            pool.wait_ge(bias_in, KT * DMA)
            pool.wait_ge(inverses_out, DMA)

            def chunk(c, slot, past, more):
                if past:
                    norm.pool_z(pool, c - 1, z[:, (slot - 1) % ZS, :, :], [KT - 1])
                    norm.pool_squares(pool, c - 1)
                if more:
                    wait_apart(pool, x_loaded, (c + 1) * KT * DMA, passed)
                    pool.tensor_scalar(rows[:, :], rows[:, :], float(D), None, ALU.add).then_inc(rows_ready, 1)
                    pool.wait_ge(lo_stored, (c + 1) * DMA)
                    slot_of["next"] = (slot + 1) % ZS
                    gather(c + 1)
                norm.pool_z(pool, c, z[:, slot, :, :], range(1, KT - 1))

            chunks(pool, chunk, ZS, 1, 1)
            norm.pool_z(pool, NCH - 1, z[:, (NCH - 1) % ZS, :, :], [KT - 1])
            norm.pool_squares(pool, NCH - 1)

        @block.vector
        def _(dve):
            dve.sem_inc(tile_used, 4)
            dve.sem_inc(divided, IR)
            norm.start_dve(dve)
            dve.wait_ge(sums_in, DMA)
            dve.reciprocal(sums, sums).then_inc(inverted, 1)

            def divide(c, tiles):
                for k in tiles:
                    if k == 0:
                        dve.wait_ge(att_loaded, (c + 1) * DMA)
                    dve.wait_ge(inv_loaded[k % IR], (c * (KT // IR) + k // IR + 1) * DMA)
                    dve.tensor_tensor(att[:, k, :], att[:, k, :], inv[:, k % IR, :], ALU.mult).then_inc(divided, 1)

            def add_tile(c, m, z_of):
                if m == 0:
                    dve.wait_ge(x_loaded, (c + 1) * KT * DMA)
                if m == KT - 1:
                    dve.wait_ge(a_used, (c + 2) * KT)
                else:
                    dve.wait_ge(tile_ready, c * (KT - 1) + m + 1)
                dve.scalar_tensor_tensor(out=z_of[:, m, :], in0=ps[:, m % 4, :], scalar=bo[:, m:m + 1],
                                         in1=z_of[:, m, :], op0=ALU.add, op1=ALU.add).then_inc(tile_used, 1)

            def scale(n, z_of):
                norm.dve_invert(dve, n)
                for i in range(NPIECE):
                    norm.dve_scale(dve, z_of, i)

            def split(n, z_of):
                for i in range(NPIECE):
                    dve.wait_ge(x_hi_done, n * NPIECE + i + 1)
                    dve.tensor_tensor(norm.piece(z_of, i), norm.piece(z_of, i), norm.piece(x_hi, i).bitcast(F32),
                                      ALU.subtract).then_inc(x_lo_done, 1)

            divide(0, range(KT))
            dve.wait_ge(bias_in, KT * DMA)

            def chunk(c, slot, past, more):
                behind = z[:, (slot - 1) % ZS, :, :]
                for k in range(KT):
                    dve.wait_ge(a_hi_done, c * KT + k + 1)
                    dve.tensor_tensor(a_lo[:, k, :], att[:, k, :], a_hi[:, k, :].bitcast(F32), ALU.subtract).then_inc(a_split, 1)
                if past:
                    add_tile(c - 1, KT - 1, behind)
                for m in range(KT - 1):
                    add_tile(c, m, z[:, slot, :, :])
                    if past and m == 1:
                        norm.dve_centre(dve, c - 1, behind)
                    if past and m == 4:
                        scale(c - 1, behind)
                    if more and 2 <= m < 6:
                        divide(c + 1, (2 * m - 4, 2 * m - 3))
                if past:
                    split(c - 1, behind)

            chunks(dve, chunk, ZS, 1, 1)
            behind = z[:, (NCH - 1) % ZS, :, :]
            add_tile(NCH - 1, KT - 1, behind)
            norm.dve_centre(dve, NCH - 1, behind)
            scale(NCH - 1, behind)
            split(NCH - 1, behind)

        @block.tensor
        def _(pe):
            norm.start_pe(pe)
            pe.sem_inc(a_used, KT)
            pe.wait_ge(const_ready, 2)

            def chunk(c, slot, past, more):
                for m in range(KT):
                    pe.wait_ge(tile_used, c * KT + m + 1)
                    for k in range(KT):
                        if m == 0:
                            pe.wait_ge(a_split, c * KT + k + 1)
                        for i, (w, a) in enumerate(((w_hi, a_hi), (w_hi, a_lo), (w_lo, a_hi))):
                            ins = pe.matmul(ps[:, m % 4, :], w[:, k, m * P:(m + 1) * P], a[:, k, :],
                                            start=(k == 0 and i == 0), stop=(k == KT - 1 and i == 2))
                        if m == KT - 1:
                            ins.then_inc(a_used, 1)
                        elif k == KT - 1:
                            ins.then_inc(tile_ready, 1)
                    if m == 1 and past:
                        norm.pe(pe, c - 1, 0)
                    if m == 4 and past:
                        norm.pe(pe, c - 1, 1)

            chunks(pe, chunk, 1, 1, 0)
            norm.pe(pe, NCH - 1, 0)
            norm.pe(pe, NCH - 1, 1)


def feed(nc, x1_hi, x1_lo, perm, up, down, eye_pair, out):
    with ExitStack() as ctx:
        def sb(name, shape, dt):
            return ctx.enter_context(nc.sbuf_tensor(name, shape, dt))

        def sem(name):
            return ctx.enter_context(nc.semaphore(name))

        MT = FM // P
        NP2 = FH // 2
        GROUPS = 4
        HPG = FH // GROUPS
        t_st = sb("t_st", [P, 2, FH, CH], F32R)
        up_hi = sb("up_hi", [P, FH, FM], F32R)
        up_lo = sb("up_lo", [P, FH, FM], F32R)
        w_dn = sb("w_dn", [P, FH, MT, FD], F32)
        eyes_in = sb("eyes_in", [P, 2, P], F32)
        eyes = sb("eyes", [P, 2, P], F32R)
        act_out = sb("act_out", [P, 4, MT, CH], F32)
        z = sb("z4", [P, ZS, KT, CH], F32)
        rows = sb("rows4", [P, KT], I32)
        ones = sb("ones4", [P, P], F32)
        ps_u = ctx.enter_context(nc.psum_tensor("ps_u", [P, 2, MT, CH], F32))
        ps_d = ctx.enter_context(nc.psum_tensor("ps_d", [P, 2, CH], F32))

        const_ready = sem("const_ready4")
        index_in = sem("index_in4")
        up_loaded = [sem(f"up_loaded{g}") for g in range(GROUPS)]
        eyes_loaded = sem("eyes_loaded")
        eyes_ready = sem("eyes_ready")
        down_in = sem("down_in")
        up_hi_done = sem("up_hi_done")
        up_split = sem("up_split")
        t_loaded = [[sem(f"t_loaded{i}_{g}") for g in range(GROUPS)] for i in range(2)]
        up_ready = sem("up_ready")
        gelu_done = sem("gelu_done")
        down_ready = sem("down_ready")
        z_added = sem("z_added")
        rows_ready = sem("rows_ready4")
        stored = sem("stored4")
        scattered = sem("scattered")
        passed = sem("passed4")
        norm = Norm(nc, ctx, ones[:, :], 2, z_added, 2)
        up_in = norm.squares[:, :, :].rearrange("p a c -> p (a c)").rearrange("p (h m) -> p h m", h=FH)
        block = ctx.enter_context(nc.Block())
        out_rows = out.rearrange("c d t -> (c d) t")

        def heads(g):
            return slice(g * HPG, (g + 1) * HPG)

        @block.sync
        def _(sp):
            def load(c, slot):
                for g in range(GROUPS):
                    for half, src in enumerate((x1_hi, x1_lo)):
                        sp.dma_start(t_st[half * FD:(half + 1) * FD, slot, heads(g), :].bitcast(F32),
                                     src[ds(c, 1), heads(g).start * FD:heads(g).stop * FD, :]
                                     .rearrange("c (h d) t -> d (c h) t", d=FD)).then_inc(t_loaded[slot][g], DMA)

            for g in range(GROUPS):
                for half in range(2):
                    sp.dma_start(up_in[half * FD:(half + 1) * FD, heads(g), :], up[heads(g)].rearrange("h d m -> d h m")).then_inc(up_loaded[g], DMA)
            load(0, 0)
            sp.dma_start(eyes_in[:, :, :], eye_pair).then_inc(eyes_loaded, DMA)
            sp.dma_start(w_dn[:, :, :, :], down.rearrange("h (m p) d -> p h m d", p=P)).then_inc(down_in, DMA)
            sp.dma_start(rows[:, :], perm).then_inc(index_in, DMA)
            load(1, 1)
            with sp.Fori(0, (NCH - 2) // 2) as it:
                for slot in range(2):
                    c = it * 2 + slot + 2
                    sp.wait_ge(down_ready, (c - 1) * NP2 + 2)
                    load(c, slot)

        @block.scalar
        def _(act):
            act.sem_inc(gelu_done, 2)
            for g in range(GROUPS):
                act.wait_ge(up_loaded[g], 2 * DMA)
                act.activation(up_hi[:, heads(g), :], up_in[:, heads(g), :], ACT.Copy).then_inc(up_hi_done, 1)
            act.wait_ge(eyes_loaded, DMA)
            act.activation(eyes[:, :, :], eyes_in[:, :, :], ACT.Copy).then_inc(eyes_ready, 1)

            def chunk(c, slot, past, more):
                behind = z[:, (slot - 1) % ZS, :, :]
                for h in range(FH):
                    act.wait_ge(up_ready, c * FH + h + 1)
                    act.wait_ge(down_ready, c * NP2 + h // 2 + 1)
                    if past == 0 and h == 0:
                        act.wait_ge(up_split, GROUPS)
                    act.activation(act_out[:, h % 4, :, :], ps_u[:, h % 2, :, :], ACT.Gelu).then_inc(gelu_done, 1)
                    if past and 3 <= h < 3 + NPIECE:
                        norm.act_square(act, c - 1, behind, h - 3)
                    if past and h == 10:
                        norm.act_root(act, c - 1)

            chunks(act, chunk, ZS, 2, 0)
            for i in range(NPIECE):
                norm.act_square(act, NCH - 1, z[:, (NCH - 1) % ZS, :, :], i)
            norm.act_root(act, NCH - 1)

        @block.gpsimd
        def _(pool):
            pool.memset(ones[:, :], 1.0).then_inc(const_ready, 1)
            pool.memset(norm.eps[:, :], EPS).then_inc(const_ready, 1)
            pool.sem_inc(scattered, ZS)
            pool.wait_ge(index_in, DMA)
            pool.sem_inc(rows_ready, 1)

            def scatter(n, slot, next_rows):
                for k in range(KT):
                    if k == 0:
                        pool.wait_ge(rows_ready, n + 1)
                    if k % PIECE == 0:
                        wait_apart(pool, norm.scaled, norm.scaled_at(n, k // PIECE), passed)
                    pool.indirect_dma_start(out_rows, bass.IndirectOffsetOnAxis(ap=rows[:, k:k + 1].bitcast(U32), axis=0),
                                            z[:, slot, k, :], None).then_inc(stored, DMA)

            def scattered_chunk(n, more):
                wait_apart(pool, stored, (n + 1) * KT * DMA, scattered)
                if more:
                    pool.tensor_scalar(rows[:, :], rows[:, :], float(D), None, ALU.add).then_inc(rows_ready, 1)

            def chunk(c, slot, past, more):
                if past:
                    norm.pool_z(pool, c - 1, z[:, (slot - 1) % ZS, :, :], [KT - 1])
                    norm.pool_squares(pool, c - 1)
                if past == 2:
                    scatter(c - 2, (slot - 2) % ZS, True)
                norm.pool_z(pool, c, z[:, slot, :, :], range(1, KT - 1))
                if past == 2:
                    scattered_chunk(c - 2, True)

            chunks(pool, chunk, ZS, 2, 0)
            norm.pool_z(pool, NCH - 1, z[:, (NCH - 1) % ZS, :, :], [KT - 1])
            norm.pool_squares(pool, NCH - 1)
            for n in (NCH - 2, NCH - 1):
                scatter(n, n % ZS, n < NCH - 1)
                scattered_chunk(n, n < NCH - 1)

        @block.vector
        def _(dve):
            dve.sem_inc(z_added, 2)
            norm.start_dve(dve)
            for g in range(GROUPS):
                dve.wait_ge(up_hi_done, g + 1)
                dve.tensor_tensor(up_lo[:, heads(g), :], up_in[:, heads(g), :], up_hi[:, heads(g), :].bitcast(F32),
                                  ALU.subtract).then_inc(up_split, 1)

            def chunk(c, slot, past, more):
                behind = z[:, (slot - 1) % ZS, :, :]
                dve.wait_ge(scattered, c + 1)
                if past:
                    copy_tile(c - 1, NP2 - 1, behind)
                    norm.dve_centre(dve, c - 1, behind)
                for i in range(NP2 - 1):
                    copy_tile(c, i, z[:, slot, :, :])
                    if past and i >= 4:
                        if i == 4:
                            norm.dve_invert(dve, c - 1)
                        for piece in ((0,), (1, 2), (3,))[i - 4]:
                            norm.dve_scale(dve, behind, piece)

            def copy_tile(c, i, z_of):
                dve.wait_ge(down_ready, c * NP2 + i + 3)
                dve.tensor_copy(z_of[:, i, :], ps_d[:, i % 2, :]).then_inc(z_added, 1)

            chunks(dve, chunk, ZS, 2, 0)
            behind = z[:, (NCH - 1) % ZS, :, :]
            copy_tile(NCH - 1, NP2 - 1, behind)
            norm.dve_centre(dve, NCH - 1, behind)
            norm.dve_invert(dve, NCH - 1)
            for i in range(NPIECE):
                norm.dve_scale(dve, behind, i)

        @block.tensor
        def _(pe):
            pe.sem_inc(down_ready, 2)
            norm.start_pe(pe)

            def down_pair(c, i, slot):
                pe.wait_ge(gelu_done, c * FH + 2 * i + 4)
                pe.wait_ge(z_added, c * NP2 + i + 1)
                for half in range(2):
                    pe.matmul(ps_d[:, i % 2, :], eyes[:, half, :], t_st[:, slot, 2 * i + half, :],
                              start=(half == 0), stop=False, skip_group_check=True)
                for m in range(MT):
                    for half in range(2):
                        h = 2 * i + half
                        ins = pe.matmul(ps_d[half * FD:(half + 1) * FD, i % 2, :], w_dn[:, h, m, :], act_out[:, h % 4, m, :],
                                        start=False, stop=(m == MT - 1), skip_group_check=True)
                ins.then_inc(down_ready, 1)

            def chunk(c, slot, past, more):
                for h in range(FH):
                    if h % HPG == 0:
                        pe.wait_ge(t_loaded[slot][h // HPG], (c // 2 + 1) * 2 * DMA)
                        if past == 0:
                            pe.wait_ge(up_split, h // HPG + 1)
                    pe.wait_ge(gelu_done, c * FH + h + 1)
                    for m in range(MT):
                        for i, w in enumerate((up_hi, up_lo)):
                            ins = pe.matmul(ps_u[:, h % 2, m, :], w[:, h, m * P:(m + 1) * P], t_st[:, slot, h, :], start=(i == 0), stop=(i == 1))
                    ins.then_inc(up_ready, 1)
                    if past == 0 and h == 3:
                        pe.wait_ge(const_ready, 2)
                        pe.wait_ge(eyes_ready, 1)
                        pe.wait_ge(down_in, DMA)
                    if h == 1 and past:
                        down_pair(c - 1, NP2 - 1, 1 - slot)
                    if h % 2 == 1 and h > 1:
                        down_pair(c, h // 2 - 1, slot)
                    if h == 3 and past:
                        norm.pe(pe, c - 1, 0)
                    if h == 10 and past:
                        norm.pe(pe, c - 1, 1)

            chunks(pe, chunk, 2, 2, 0)
            down_pair(NCH - 1, NP2 - 1, (NCH - 1) % 2)
            norm.pe(pe, NCH - 1, 0)
            norm.pe(pe, NCH - 1, 1)


def build(nc, arrays, phases=4):
    def given(name):
        a = arrays[name]
        return nc.dram_tensor(name, a.shape, mybir.dt.from_np(a.dtype), kind="ExternalInput").ap()

    def kept(name, shape):
        return nc.dram_tensor(name, shape, F32, kind="Internal").ap()

    g = {name: given(name) for name in arrays}
    out = nc.dram_tensor("out_0_dram", [NCH, D, CH], F32, kind="ExternalOutput").ap()
    qk_halves = kept("qk_halves", [B, H + KV, 4, HALF, S])
    v_keys = kept("v_keys", [B, KV, P, S // P, HD])
    att_o = kept("att_o", [B, H, HD, S])
    att_l = kept("att_l", [B, H, S])
    att_inv = kept("att_inv", [B, H, S])
    x1_hi = kept("x1_hi", [NCH, D, CH])
    x1_lo = kept("x1_lo", [NCH, D, CH])
    project(nc, g["x_chunks"], g["wqkvT"], g["bias_qk"], g["bias_v"], g["cos"], g["sin"], qk_halves, v_keys)
    with ExitStack() as ctx:
        wo_hi = ctx.enter_context(nc.sbuf_tensor("wo_hi", [P, KT, D], F32R))
        wo_lo = ctx.enter_context(nc.sbuf_tensor("wo_lo", [P, KT, D], F32R))
        if phases >= 2:
            attend(nc, qk_halves, v_keys, g["identity"], g["w_o"], g["perm"], wo_hi, wo_lo, att_o, att_l)
        if phases >= 3:
            mix(nc, g["x_chunks"], att_o, att_l, att_inv, wo_hi, wo_lo, g["bias_o"], g["perm"], x1_hi, x1_lo)
    if phases >= 4:
        feed(nc, x1_hi, x1_lo, g["perm"], g["up"], g["down"], g["eye_pair"], out)


def host_layout(L0_attn_x, L0_attn_w_qkv, L0_attn_b_qkv, L0_attn_w_o, L0_attn_b_o, L0_ffn_up, L0_ffn_down, L0_ffn_perm):
    c = np.ascontiguousarray
    rows = np.arange((H + KV) * HD).reshape(QK_PAIRS, HPT, HALF, 2).transpose(0, 3, 1, 2).reshape(-1)
    perm = np.asarray(L0_ffn_perm)
    order = np.concatenate([rows, np.arange((H + KV) * HD, (H + 2 * KV) * HD)])
    inv_freq = np.float32(1.0) / np.power(np.float32(10000.0), np.arange(0, HD, 2, dtype=np.float32) / np.float32(HD))
    angle = np.arange(S, dtype=np.float32)[None, :] * inv_freq[:, None]
    return {
        "x_chunks": c(np.asarray(L0_attn_x).reshape(NCH, CH, D).transpose(0, 2, 1)),
        "wqkvT": c(np.asarray(L0_attn_w_qkv)[order].T),
        "bias_qk": c(np.asarray(L0_attn_b_qkv)[rows].reshape(2 * QK_PAIRS, P).T),
        "bias_v": c(np.asarray(L0_attn_b_qkv)[(H + KV) * HD:]),
        "w_o": c(np.asarray(L0_attn_w_o)),
        "bias_o": c(np.asarray(L0_attn_b_o).reshape(D, 1)),
        "up": c(np.asarray(L0_ffn_up)),
        "down": c(np.asarray(L0_ffn_down)),
        "perm": c(perm.reshape(KT, P).T),
        "cos": c(np.tile(np.cos(angle.astype(np.float64)).astype(np.float32), (HPT, 1))),
        "sin": c(np.tile(np.sin(angle.astype(np.float64)).astype(np.float32), (HPT, 1))),
        "identity": np.eye(P, dtype=np.float32),
        "eye_pair": c(np.tile(np.eye(P, dtype=np.float32).reshape(P // FD, FD, P).transpose(1, 0, 2), (P // FD, 1, 1))),
    }


def result(chunks):
    return np.ascontiguousarray(chunks.transpose(0, 2, 1).reshape(B, S, D))


def kernel(**inputs):
    import concourse.bacc as bacc
    from concourse.bass_utils import run_bass_kernel_spmd

    arrays = host_layout(**{name: np.asarray(a) for name, a in inputs.items()})
    nc = bacc.Bacc("TRN2", target_bir_lowering=False, num_devices=1)
    build(nc, arrays)
    r = run_bass_kernel_spmd(nc, [arrays], core_ids=[0])
    return result(r.results[0]["out_0_dram"])
```

```python
from contextlib import ExitStack

import concourse.bass as bass
import numpy as np
from concourse import mybir
from concourse.alu_op_type import AluOpType as ALU

F32 = mybir.dt.float32
F32R = mybir.dt.float32r
I32 = mybir.dt.int32
U32 = mybir.dt.uint32
ACT = mybir.ActivationFunctionType
AX = mybir.AxisListType

P = 128
B, S, D = 2, 2048, 1024
T = B * S
H, KV, HD = 32, 8, 32
HALF = HD // 2
CH = 512
NCH = T // CH
CPB = S // CH
KT = D // P
NKV = KV * HD
QK_PAIRS = (H + KV) * HALF // P
HPT = P // HALF
EPS = 1e-5
LOWEST = -3.0e38
FH, FD, FM = 16, 64, 256
DMA = 16


def ds(start, size):
    return bass.ds(start, size)


def wait_apart(eng, sem, value, passed):
    eng.wait_ge(sem, value)
    eng.sem_inc(passed, 1)


def project(nc, x_chunks, wqkvT, bias_qk, bias_v, cos, sin, qk_halves, v_keys):
    with ExitStack() as ctx:
        def sb(name, shape, dt):
            return ctx.enter_context(nc.sbuf_tensor(name, shape, dt))

        def sem(name):
            return ctx.enter_context(nc.semaphore(name))

        NW = 2 * QK_PAIRS * P + NKV
        WC = 2 * P
        NB = NW // WC
        w_hi = sb("w_hi", [P, KT, NW], F32R)
        w_lo = sb("w_lo", [P, KT, NW], F32R)
        x_in = sb("x_in", [P, KT, CH], F32)
        w_in = sb("w_in", [P, 2, KT // 2, WC], F32)
        x_hi = sb("x_hi", [P, 2, KT, CH], F32R)
        x_lo = sb("x_lo", [P, 2, KT, CH], F32R)
        trig = sb("trig", [P, 2, CH], F32)
        prod = sb("prod", [P, 4, CH], F32)
        rot = prod[:, 0:2, :]
        halves = sb("halves", [P, 4, CH], F32R)
        v_out = sb("v_out", [P, 2, NKV], F32)
        bqk = sb("bqk", [P, 2 * QK_PAIRS], F32)
        bv = sb("bv", [P, NKV], F32)
        ps_qk = ctx.enter_context(nc.psum_tensor("ps_qk", [P, 2, 2, CH], F32))
        ps_v = ctx.enter_context(nc.psum_tensor("ps_v", [P, 2, CH], F32))

        bias_in = sem("bias_in")
        w_loaded = [sem(f"w_loaded{i}") for i in range(2)]
        w_hi_done = sem("w_hi_done")
        w_split = sem("w_split")
        x_loaded = sem("x_loaded")
        x_hi_done = sem("x_hi_done")
        x_split = sem("x_split")
        trig_loaded = sem("trig_loaded")
        qk_ready = sem("qk_ready")
        rope_mul = sem("rope_mul")
        rope_sum = sem("rope_sum")
        rope_hi = sem("rope_hi")
        rope_lo = sem("rope_lo")
        qk_stored = sem("qk_stored")
        v_ready = sem("v_ready")
        v_added = sem("v_added")
        v_stored = [sem(f"v_stored{i}") for i in range(2)]
        block = ctx.enter_context(nc.Block())
        ITER = NCH // 2

        def rows_of(n):
            return slice(n % 2 * (KT // 2), (n % 2 + 1) * (KT // 2))

        def cols_of(n):
            return slice(n // 2 * WC, (n // 2 + 1) * WC)

        @block.sync
        def _(sp):
            def load_x(c):
                sp.dma_start(x_in[:, :, :], x_chunks[ds(c, 1)].rearrange("c (k p) t -> p (c k) t", p=P)).then_inc(x_loaded, DMA)

            sp.dma_start(bqk[:, :], bias_qk).then_inc(bias_in, DMA)
            sp.dma_start(bv[:, :], bias_v.rearrange("(a n) -> a n", a=1).to_broadcast([P, NKV])).then_inc(bias_in, DMA)
            load_x(0)
            for n in range(2 * NB):
                if n >= 2:
                    sp.wait_ge(w_split, n - 1)
                sp.dma_start(w_in[:, n % 2, :, :], wqkvT[rows_of(n % 2).start * P:rows_of(n % 2).stop * P, cols_of(n)]
                             .rearrange("(k p) n -> p k n", p=P)).then_inc(w_loaded[n % 2], DMA)
            sp.sem_inc(qk_stored, 4 * DMA)
            for i in range(2):
                sp.sem_inc(v_stored[i], DMA)
            with sp.Fori(0, ITER) as it:
                for u in range(2):
                    c = it * 2 + u
                    tok = (c % CPB) * CH
                    sp.wait_ge(rope_mul, c * QK_PAIRS + 2)
                    sp.dma_start(trig[:, 0, :], cos[:, ds(tok, CH)]).then_inc(trig_loaded, DMA)
                    sp.dma_start(trig[:, 1, :], sin[:, ds(tok, CH)]).then_inc(trig_loaded, DMA)
                    sp.wait_ge(x_split, c + 1)
                    load_x((c + 1) % NCH)
                    for j in range(QK_PAIRS):
                        sp.wait_ge(rope_lo, c * QK_PAIRS + j + 2)
                        for v in range(4):
                            sp.dma_start(qk_halves[ds(c // CPB, 1), j * HPT:(j + 1) * HPT, v, :, ds(tok, CH)]
                                         .rearrange("b h i t -> (b h) i t"),
                                         halves[:, v, :].bitcast(F32)).then_inc(qk_stored, DMA)
                    for t in range(CH // P):
                        sp.wait_ge(v_added, c * 4 + t + 5)
                        sp.dma_start(v_keys[ds(c // CPB, 1), :, :, ds((c % CPB) * 4 + t, 1), :]
                                     .rearrange("b g p k d -> p (b g) (k d)"),
                                     v_out[:, t % 2, :].rearrange("p (g d) -> p g d", d=HD)).then_inc(v_stored[t % 2], DMA)
            sp.wait_ge(qk_stored, 4 * DMA * (NCH * QK_PAIRS + 1))
            for i in range(2):
                sp.wait_ge(v_stored[i], DMA * (NCH * 2 + 1))
            sp.wait_ge(x_loaded, DMA * (NCH + 1))

        @block.scalar
        def _(act):
            def split_w(n):
                act.wait_ge(w_loaded[n % 2], DMA * (n // 2 + 1))
                act.activation(w_hi[:, rows_of(n), cols_of(n)], w_in[:, n % 2, :, :], ACT.Copy).then_inc(w_hi_done, 1)

            def split_x(c, u):
                act.wait_ge(x_loaded, (c + 1) * DMA)
                act.wait_ge(v_ready, c * 2)
                act.activation(x_hi[:, u, :, :], x_in[:, :, :], ACT.Copy).then_inc(x_hi_done, 1)

            split_w(0)
            split_w(1)
            act.wait_ge(x_loaded, DMA)
            act.activation(x_hi[:, 0, :, :], x_in[:, :, :], ACT.Copy).then_inc(x_hi_done, 1)
            for n in range(2, 2 * NB):
                split_w(n)
            with act.Fori(0, ITER) as it:
                for u in range(2):
                    c = it * 2 + u
                    for j in range(QK_PAIRS):
                        n = c * QK_PAIRS + j
                        if j == 2:
                            split_x(c + 1, 1 - u)
                        act.wait_ge(rope_sum, 2 * n + 2)
                        act.wait_ge(qk_stored, (n + 1) * 4 * DMA)
                        act.activation(halves[:, 0:2, :], rot, ACT.Copy).then_inc(rope_hi, 1)

        @block.gpsimd
        def _(pool):
            pool.sem_inc(rope_lo, 1)
            with pool.Fori(0, ITER) as it:
                for u in range(2):
                    for j in range(QK_PAIRS):
                        n = (it * 2 + u) * QK_PAIRS + j
                        pool.wait_ge(rope_mul, n + 3)
                        pool.tensor_tensor(prod[:, 0, :], prod[:, 0, :], prod[:, 2, :], ALU.subtract).then_inc(rope_sum, 1)
                        pool.tensor_tensor(prod[:, 1, :], prod[:, 1, :], prod[:, 3, :], ALU.add).then_inc(rope_sum, 1)
                        pool.wait_ge(rope_hi, n + 1)
                        pool.tensor_tensor(halves[:, 2:4, :], rot, halves[:, 0:2, :].bitcast(F32), ALU.subtract).then_inc(rope_lo, 1)

        @block.vector
        def _(dve):
            dve.sem_inc(rope_mul, 2)
            dve.sem_inc(v_added, 4)

            def split_w(n):
                dve.wait_ge(w_hi_done, n + 1)
                dve.tensor_tensor(w_lo[:, rows_of(n), cols_of(n)], w_in[:, n % 2, :, :], w_hi[:, rows_of(n), cols_of(n)].bitcast(F32),
                                  ALU.subtract).then_inc(w_split, 1)

            def split_x(c, u):
                dve.wait_ge(x_hi_done, c + 1)
                dve.tensor_tensor(x_lo[:, u, :, :], x_in[:, :, :], x_hi[:, u, :, :].bitcast(F32), ALU.subtract).then_inc(x_split, 1)

            split_w(0)
            split_w(1)
            split_x(0, 0)
            for n in range(2, 2 * NB):
                split_w(n)
            dve.wait_ge(bias_in, 2 * DMA)
            with dve.Fori(0, ITER) as it:
                for u in range(2):
                    c = it * 2 + u
                    for j in range(QK_PAIRS):
                        n = c * QK_PAIRS + j
                        if j == 3:
                            split_x(c + 1, 1 - u)
                        if j == 0:
                            dve.wait_ge(trig_loaded, (c + 1) * 2 * DMA)
                        dve.wait_ge(qk_ready, n + 1)
                        dve.wait_ge(rope_lo, n + 1)
                        for k, (part, table) in enumerate(((0, 0), (1, 0), (1, 1), (0, 1))):
                            ins = dve.scalar_tensor_tensor(
                                out=prod[:, k, :], in0=ps_qk[:, j % 2 if u == 0 else (j + QK_PAIRS) % 2, part, :],
                                scalar=bqk[:, 2 * j + part:2 * j + part + 1], in1=trig[:, table, :],
                                op0=ALU.add, op1=ALU.mult)
                        ins.then_inc(rope_mul, 1)
                    for t in range(CH // P):
                        if t % 2 == 0:
                            dve.wait_ge(v_ready, c * 2 + t // 2 + 3)
                        dve.wait_ge(v_stored[t % 2], (c * 2 + t // 2 + 1) * DMA)
                        dve.tensor_tensor(v_out[:, t % 2, :], ps_v[:, t // 2, (t % 2) * NKV:(t % 2 + 1) * NKV],
                                          bv[:, :], ALU.add).then_inc(v_added, 1)

        @block.tensor
        def _(pe):
            pe.sem_inc(v_ready, 2)
            with pe.Fori(0, ITER) as it:
                for u in range(2):
                    c = it * 2 + u
                    pe.wait_ge(x_split, c + 1)
                    for j in range(QK_PAIRS):
                        n = c * QK_PAIRS + j
                        pe.wait_ge(w_split, 2 * (j + 1))
                        pe.wait_ge(rope_mul, n + 1)
                        for part in range(2):
                            cols = slice((2 * j + part) * P, (2 * j + part + 1) * P)
                            terms = [(w, x, k) for k in range(KT) for w, x in ((w_hi, x_hi), (w_hi, x_lo), (w_lo, x_hi))]
                            for i, (w, x, k) in enumerate(terms):
                                ins = pe.matmul(ps_qk[:, j % 2 if u == 0 else (j + QK_PAIRS) % 2, part, :], w[:, k, cols], x[:, u, k, :],
                                                start=(i == 0), stop=(i == len(terms) - 1))
                        ins.then_inc(qk_ready, 1)
                    pe.wait_ge(w_split, 2 * NB)
                    for t in range(CH // P):
                        if t % 2 == 0:
                            pe.wait_ge(v_added, c * 4 + t + 2)
                        cols = slice(2 * QK_PAIRS * P, NW)
                        terms = [(w, x, k) for k in range(KT) for w, x in ((w_hi, x_hi), (w_lo, x_hi), (w_hi, x_lo))]
                        for i, (w, x, k) in enumerate(terms):
                            ins = pe.matmul(ps_v[:, t // 2, (t % 2) * NKV:(t % 2 + 1) * NKV],
                                            x[:, u, k, t * P:(t + 1) * P], w[:, k, cols],
                                            start=(i == 0), stop=(i == len(terms) - 1))
                        if t % 2 == 1:
                            ins.then_inc(v_ready, 1)


QT = S // P
SLOTS = 2
NPAIR = B * H // 2
STEPS = [(c, kt) for c in range(CPB) for kt in range((c + 1) * CH // P)]
NSTEP = len(STEPS)
CHUNK_END = [STEPS.index((c, (c + 1) * CH // P - 1)) + 1 for c in range(CPB)]
ROWS = 3 * HD
RING = 4
OB, MB = 1, 3
TPC = CH // P
ROWS_AFTER = 5
LEAD = 17
LAG = 2


def units_of_maxima():
    units = []
    for c in range(CPB):
        mine = [(j, t, g) for t in range(c * TPC, (c + 1) * TPC) for g in range(c + 1) for j in range(2)]
        if c:
            mine.insert(ROWS_AFTER, ("rows", c - 1))
        units += mine
    return units + [("rows", CPB - 1)]


UNITS = units_of_maxima()
NUNIT = len(UNITS)
assert NUNIT % MB == 0


def units_before(step):
    width = [CH - max(kt * P - c * CH, 0) for c, kt in STEPS]
    width = width[LEAD:] + width[:LEAD]
    return NUNIT if step == NSTEP else (NUNIT - 1) * sum(width[:step]) // sum(width[:-1])


EARLY = units_before(NSTEP - LEAD)


def units_at(step):
    own = range(units_before(NSTEP - LEAD + step), units_before(NSTEP - LEAD + step + 1)) if step < LEAD else ()
    nxt = range(units_before(step - LEAD), units_before(step - LEAD + 1)) if step >= LEAD else ()
    return own, nxt


BETWEEN = {0: (0, 0, 0, 0), 1: (0, 0, 0, 1), 2: (0, 1, 0, 1), 3: (1, 1, 0, 1), 4: (1, 1, 1, 1)}
EARLY_ROWS = [c for c in range(CPB) if UNITS.index(("rows", c)) < EARLY]


def attend(nc, qk_halves, v_keys, identity, w_o, perm, wo_hi, wo_lo, att_o, att_l, att_inv):
    with ExitStack() as ctx:
        def sb(name, shape, dt):
            return ctx.enter_context(nc.sbuf_tensor(name, shape, dt))

        def sem(name):
            return ctx.enter_context(nc.semaphore(name))

        q_st = sb("q_st", [P, SLOTS, 2, S], F32R)
        k_st = sb("k_st", [P, SLOTS, S], F32R)
        v_st = sb("v_st", [P, SLOTS, QT, 2 * HD], F32)
        probs = sb("probs", [P, RING, 2, CH], F32)
        o_sb = sb("o_sb", [P, 2, CH], F32)
        ident = sb("ident", [P, P], F32)
        causal = sb("causal", [P, CH], F32)
        scratch = sb("scratch", [P, MB, CH], F32)
        part_max = sb("part_max", [P, 2, QT, CPB], F32)
        neg_max = sb("neg_max", [P, 2, TPC], F32)
        max_halves = sb("max_halves", [P, 2, 2, TPC], F32R)
        max_rows = sb("max_rows", [2 * 2 * TPC, P], F32R)
        sums = sb("sums", [P, CH], F32)
        wo_rows = sb("wo_rows", [P, KT], I32)
        wo_in = sb("wo_in", [P, KT, D], F32)
        ps_s = ctx.enter_context(nc.psum_tensor("ps_s", [P, 2, 2, CH], F32))
        ps_o = ctx.enter_context(nc.psum_tensor("ps_o", [P, OB, CH], F32))
        ps_m = ctx.enter_context(nc.psum_tensor("ps_m", [P, MB, CH], F32))

        causal_ready = sem("causal_ready")
        ones_ready = sem("ones_ready")
        ident_in = sem("ident_in")
        loaded = [sem(f"loaded{i}") for i in range(SLOTS)]
        s_ready = sem("s_ready")
        exp_done = sem("exp_done")
        masked = sem("masked")
        pv_done = sem("pv_done")
        o_copied = sem("o_copied")
        o_stored = [sem(f"o_stored{i}") for i in range(2)]
        m_ready = sem("m_ready")
        m_used = sem("m_used")
        max_step = sem("max_step")
        rows_loaded = sem("rows_loaded")
        dve_passed = sem("dve_passed")
        pool_passed = sem("pool_passed")
        block = ctx.enter_context(nc.Block())
        sums_in = sem("sums_in")
        inverted = sem("inverted")
        inverses_out = sem("inverses_out")
        wo_index_in = sem("wo_index_in")
        wo_gathered = sem("wo_gathered")
        wo_turned = sem("wo_turned")
        wo_hi_done = sem("wo_hi_done")
        wo_split = sem("wo_split")
        WO_BANKS = [(k, m) for k in range(KT) for m in range(0, D, CH)]
        NDIAG = CPB * TPC
        LOADS = 7
        ROW_LOADS = 4

        def stages(eng, stage):
            with eng.Fori(0, NPAIR // 2 - 1) as it:
                for s in range(SLOTS):
                    stage(it, s, True)
            stage(NPAIR // 2 - 1, 0, True, invert=True)
            stage(NPAIR // 2 - 1, 1, False)

        @block.sync
        def _(sp):
            def where(it, s):
                return it // KV, it % KV, (it % KV) * 4 + 2 * s

            def load(it, s):
                b, g, h = where(it, s)
                head = qk_halves[ds(b, 1), ds(g + H, 1)].rearrange("b h v i t -> (b h v i) t")
                sp.dma_start(k_st[0:2 * HD, s, :].bitcast(F32), head).then_inc(loaded[s], DMA)
                sp.dma_start(k_st[2 * HD:3 * HD, s, :].bitcast(F32), head[0:HD, :]).then_inc(loaded[s], DMA)
                for j in range(2):
                    head = qk_halves[ds(b, 1), ds(h + j, 1)].rearrange("b h v i t -> (b h v i) t")
                    sp.dma_start(q_st[0:HD, s, j, :].bitcast(F32), head[0:HD, :]).then_inc(loaded[s], DMA)
                    sp.dma_start(q_st[HD:3 * HD, s, j, :].bitcast(F32), head).then_inc(loaded[s], DMA)
                sp.dma_start(v_st[:, s, :, 0:HD], v_keys[ds(b, 1), ds(g, 1)].rearrange("b g p k d -> (b g p) k d")).then_inc(loaded[s], DMA)

            def load_rows(p, s, c):
                sp.wait_ge(m_used, p * NUNIT + UNITS.index(("rows", c)) + 1 + MB)
                for half in range(2):
                    for j in range(2):
                        first = (2 * half + j) * TPC
                        sp.dma_start(q_st[ROWS + half:ROWS + half + 1, s, j, c * CH:(c + 1) * CH].rearrange("a (t q) -> a t q", q=P).bitcast(F32),
                                     max_rows[first:first + TPC, :].bitcast(F32)).then_inc(rows_loaded, DMA)

            def store_o(it, s, p, c):
                b, _, h = where(it, s)
                sp.wait_ge(o_copied, p * CPB + c + 1 + OB)
                for j in range(2):
                    first = 2 * HD * j
                    sp.dma_start(att_o[ds(b, 1), ds(h + j, 1), :, c * CH:(c + 1) * CH].rearrange("b h d t -> (b h d) t"),
                                 o_sb[first:first + HD, c % 2, :]).then_inc(o_stored[c % 2], DMA)
                    sp.dma_start(att_l[ds(b, 1), ds(h + j, 1), c * CH:(c + 1) * CH].rearrange("b h t -> (b h) t"),
                                 o_sb[first + HD:first + HD + 1, c % 2, :]).then_inc(o_stored[c % 2], DMA)

            sp.dma_start(wo_rows[:, :], perm).then_inc(wo_index_in, DMA)
            sp.dma_start(ident[:, :], identity).then_inc(ident_in, DMA)
            for i in range(2):
                sp.sem_inc(o_stored[i], 4 * DMA)
            sp.sem_inc(rows_loaded, ROW_LOADS * DMA)
            load(0, 0)
            for c in EARLY_ROWS:
                load_rows(0, 0, c)

            def stage(it, s, more, invert=False):
                p = it * 2 + s
                late = [c for c in range(CPB) if c not in EARLY_ROWS]
                load_rows(p, s, late[0])
                if more:
                    sp.wait_ge(pv_done, p * NSTEP + RING)
                    load(*((it, 1) if s == 0 else (it + 1, 0)))
                if invert:
                    for i in range(2):
                        sp.wait_ge(o_stored[i], 4 * DMA * (NPAIR // B * CPB // 2 + 1))
                    sp.dma_start(sums[:, :], att_l[0].rearrange("h (q t) -> (h q) t", t=CH)).then_inc(sums_in, DMA)
                store_o(it, s, p, 0)
                store_o(it, s, p, 1)
                for c in late[1:]:
                    load_rows(p, s, c)
                for c in EARLY_ROWS[:1] if more else ():
                    load_rows(p + 1, 1 - s, c)
                store_o(it, s, p, 2)
                for c in EARLY_ROWS[1:] if more else ():
                    load_rows(p + 1, 1 - s, c)
                if invert:
                    sp.wait_ge(inverted, 1)
                    sp.dma_start(att_inv[0].rearrange("h (q t) -> (h q) t", t=CH), sums[:, :]).then_inc(inverses_out, DMA)
                store_o(it, s, p, 3)

            stages(sp, stage)
            for i in range(2):
                sp.wait_ge(o_stored[i], 4 * DMA * (NPAIR * CPB // 2 + 1))
            sp.wait_ge(inverses_out, DMA)

        @block.scalar
        def _(act):
            act.sem_inc(exp_done, 2)
            act.sem_inc(o_copied, OB)
            for i, (k, m) in enumerate(WO_BANKS):
                act.wait_ge(wo_turned, i + 1)
                act.activation(wo_hi[:, k, m:m + CH], ps_s[:, i // 2 % 2, i % 2, :], ACT.Copy).then_inc(wo_hi_done, 1)

            def copy_o(p, c):
                act.wait_ge(pv_done, p * NSTEP + CHUNK_END[c] + RING)
                act.wait_ge(o_stored[c % 2], (p * 2 + c // 2 + 1) * 4 * DMA)
                act.activation(o_sb[:, c % 2, :], ps_o[:, c % OB, :], ACT.Copy).then_inc(o_copied, 1)

            def stage(it, s, more, invert=False):
                p = it * 2 + s
                for n, (c, kt) in enumerate(STEPS):
                    off = max(kt * P - c * CH, 0)
                    act.wait_ge(s_ready, p * NSTEP + n + 1)
                    act.wait_ge(pv_done, p * NSTEP + n + 1)
                    act.activation(probs[:, n % RING, :, off:CH], ps_s[:, n % 2, :, off:CH], ACT.Exp,
                                   scale=HD ** -0.5).then_inc(exp_done, 1)
                    if c and kt == 0:
                        copy_o(p, c - 1)
                copy_o(p, CPB - 1)

            stages(act, stage)

        @block.gpsimd
        def _(pool):
            def stage(it, s, more, invert=False):
                p = it * 2 + s
                for n, (c, kt) in enumerate(STEPS):
                    off = kt * P - c * CH
                    if off >= 0:
                        wait_apart(pool, exp_done, p * NSTEP + n + 3, pool_passed)
                        diagonal = probs[:, n % RING, :, off:off + P]
                        pool.affine_select(out=diagonal, in_=diagonal, compare_op=ALU.is_ge, fill=0.0, base=0,
                                           pattern=[[0, 2], [1, P]], channel_multiplier=-1).then_inc(masked, 1)

            pool.memset(causal[:, :], 0.0).then_inc(causal_ready, 1)
            pool.wait_ge(causal_ready, 1)
            pool.affine_select(out=causal[:, CH - P:CH], in_=causal[:, CH - P:CH], compare_op=ALU.is_ge, fill=LOWEST,
                               base=0, pattern=[[-1, P]], channel_multiplier=1).then_inc(causal_ready, 1)
            pool.wait_ge(wo_index_in, DMA)
            pool.wait_ge(loaded[0], LOADS * DMA)
            for k in range(KT):
                pool.indirect_dma_start(wo_in[:, k, :], None, w_o,
                                        bass.IndirectOffsetOnAxis(ap=wo_rows[:, k:k + 1].bitcast(U32), axis=0)).then_inc(wo_gathered, DMA)
            stages(pool, stage)

        @block.vector
        def _(dve):
            dve.sem_inc(m_used, MB)
            dve.memset(part_max[:, :, :, :], LOWEST)
            dve.memset(k_st[ROWS:ROWS + 2, :, :].bitcast(F32), 1.0)
            dve.memset(v_st[:, :, :, HD:2 * HD], 1.0).then_inc(ones_ready, 1)
            dve.wait_ge(ones_ready, 1)
            dve.wait_ge(causal_ready, 2)

            def unit(p, n):
                j, t, g = UNITS[n]
                w = min(CH, (t + 1) * P - g * CH)
                if g == t * P // CH:
                    wait_apart(dve, m_ready, p * NUNIT + n + 1, dve_passed)
                    dve.tensor_tensor_reduce(scratch[:, n % MB, 0:w], ps_m[:, n % MB, 0:w], causal[:, CH - w:CH], 1.0, LOWEST,
                                             ALU.add, ALU.max, part_max[:, j, t, g:g + 1]).then_inc(m_used, 1)
                else:
                    dve.wait_ge(m_ready, p * NUNIT + n + 1)
                    dve.tensor_reduce(part_max[:, j, t, g:g + 1], ps_m[:, n % MB, 0:w], AX.X, ALU.max).then_inc(m_used, 1)
                if n + 1 < NUNIT and (j, t, g) == (1, (c := t // TPC) * TPC + TPC - 1, c):
                    finish(p, c, n)

            def finish(p, c, n):
                done = (p * CPB + c) * 3
                dve.wait_ge(m_used, p * NUNIT + n + 1 + MB)
                dve.tensor_reduce(neg_max[:, :, :], part_max[:, :, c * TPC:(c + 1) * TPC, :], AX.X, ALU.max, negate=True).then_inc(max_step, 1)
                dve.wait_ge(max_step, done + 1)
                dve.tensor_copy(max_halves[:, 0, :, :], neg_max[:, :, :]).then_inc(max_step, 1)
                dve.wait_ge(max_step, done + 2)
                dve.tensor_tensor(max_halves[:, 1, :, :], neg_max[:, :, :], max_halves[:, 0, :, :].bitcast(F32),
                                  ALU.subtract).then_inc(max_step, 1)

            def rows(p, n):
                dve.wait_ge(rows_loaded, ROW_LOADS * DMA * (p * CPB + UNITS[n][1] + 1))
                dve.wait_ge(m_ready, p * NUNIT + n + 1)
                dve.tensor_copy(max_rows[:, :], ps_m[0:4 * TPC, n % MB, 0:P]).then_inc(m_used, 1)

            def maxima(p, ns):
                for n in ns:
                    (rows if UNITS[n][0] == "rows" else unit)(p, n)

            maxima(0, range(EARLY))
            for i, (k, m) in enumerate(WO_BANKS):
                dve.wait_ge(wo_hi_done, i + 1)
                dve.tensor_tensor(wo_lo[:, k, m:m + CH], ps_s[:, i // 2 % 2, i % 2, :], wo_hi[:, k, m:m + CH].bitcast(F32),
                                  ALU.subtract).then_inc(wo_split, 1)

            def stage(it, s, more, invert=False):
                p = it * 2 + s
                for step in range(NSTEP):
                    own, nxt = units_at(step)
                    maxima(p, own)
                    if more:
                        maxima(p + 1, nxt)
                    if invert and step == NSTEP // 2:
                        dve.wait_ge(sums_in, DMA)
                        dve.reciprocal(sums[:, :], sums[:, :]).then_inc(inverted, 1)

            stages(dve, stage)

        @block.tensor
        def _(pe):
            def unit(p, s, n):
                pe.wait_ge(m_used, p * NUNIT + n + 1)
                if UNITS[n][0] == "rows":
                    pe.wait_ge(max_step, (p * CPB + UNITS[n][1]) * 3 + 3)
                    pe.transpose(ps_m[0:4 * TPC, n % MB, 0:P], max_halves[:, :, :, :].rearrange("p a j t -> p (a j t)").bitcast(F32),
                                 ident[:, :]).then_inc(m_ready, 1)
                else:
                    j, t, g = UNITS[n]
                    w = min(CH, (t + 1) * P - g * CH)
                    pe.matmul(ps_m[:, n % MB, 0:w], q_st[0:ROWS, s, j, t * P:(t + 1) * P],
                              k_st[0:ROWS, s, g * CH:g * CH + w], start=True, stop=True).then_inc(m_ready, 1)

            pe.sem_inc(pv_done, RING)
            pe.wait_ge(ident_in, DMA)
            pe.wait_ge(ones_ready, 1)
            pe.wait_ge(loaded[0], LOADS * DMA)
            for n in range(EARLY):
                unit(0, 0, n)
            pe.wait_ge(wo_gathered, KT * DMA)
            for i, (k, m) in enumerate(WO_BANKS):
                if i >= 4:
                    pe.wait_ge(wo_split, i - 3)
                for t in range(CH // P):
                    ins = pe.transpose(ps_s[:, i // 2 % 2, i % 2, t * P:(t + 1) * P], wo_in[:, m // P + t, k * P:(k + 1) * P], ident[:, :])
                ins.then_inc(wo_turned, 1)
            pe.wait_ge(wo_split, len(WO_BANKS))

            def stage(it, s, more, invert=False):
                p = it * 2 + s

                def scores(n, j):
                    c, kt = STEPS[n]
                    off = max(kt * P - c * CH, 0)
                    if j == 0:
                        if kt == 0:
                            pe.wait_ge(rows_loaded, (p * CPB + c + 2) * ROW_LOADS * DMA)
                        pe.wait_ge(exp_done, p * NSTEP + n + 1)
                    ins = pe.matmul(ps_s[:, n % 2, j, off:CH], k_st[0:ROWS + 2, s, kt * P:(kt + 1) * P],
                                    q_st[0:ROWS + 2, s, j, c * CH + off:(c + 1) * CH], start=True, stop=True)
                    if j == 1:
                        ins.then_inc(s_ready, 1)

                def values(n, j):
                    c, kt = STEPS[n]
                    off = max(kt * P - c * CH, 0)
                    if j == 0:
                        if kt == 0:
                            pe.wait_ge(o_copied, p * CPB + c + 1)
                        pe.wait_ge(exp_done, p * NSTEP + n + 3)
                        if kt * P >= c * CH:
                            pe.wait_ge(masked, p * NDIAG + sum(b * P >= a * CH for a, b in STEPS[:n + 1]))
                    ins = pe.matmul(ps_o[2 * HD * j:2 * HD * (j + 1), c % OB, off:CH], v_st[:, s, kt, :],
                                    probs[:, n % RING, j, off:CH], start=(kt == 0), stop=(n + 1 in CHUNK_END),
                                    skip_group_check=True)
                    if j == 1:
                        ins.then_inc(pv_done, 1)

                for n in range(NSTEP + LAG):
                    units = []
                    if n < NSTEP:
                        own, nxt = units_at(n)
                        units = [(p, s, m) for m in own] + [(p + 1, 1 - s, m) for m in nxt if more]
                    if n == LEAD and more:
                        pe.wait_ge(loaded[1 - s], (it + 1 if s == 0 else it + 2) * LOADS * DMA)
                    for slot, after in enumerate(BETWEEN[min(len(units), 4)]):
                        if n < NSTEP and slot < 2:
                            scores(n, slot)
                        if n >= LAG and slot >= 2:
                            values(n - LAG, slot - 2)
                        for which in units[:after]:
                            unit(*which)
                        units = units[after:]
                    for which in units:
                        unit(*which)

            stages(pe, stage)


PIECE = 2
NPIECE = KT // PIECE


class Norm:

    def __init__(self, nc, ctx, ones, number, added, ahead):
        def sem(name):
            return ctx.enter_context(nc.semaphore(f"{name}_{number}"))

        self.ones, self.added, self.ahead = ones, added, ahead
        self.squares = ctx.enter_context(nc.sbuf_tensor(f"norm_squares_{number}", [P, KT, CH], F32))
        self.total = ctx.enter_context(nc.sbuf_tensor(f"norm_total_{number}", [P, 2, CH], F32))
        self.mean = ctx.enter_context(nc.sbuf_tensor(f"norm_mean_{number}", [P, CH], F32))
        self.root = ctx.enter_context(nc.sbuf_tensor(f"norm_root_{number}", [P, CH], F32))
        self.eps = ctx.enter_context(nc.sbuf_tensor(f"norm_eps_{number}", [P, 1], F32))
        self.psum = ctx.enter_context(nc.psum_tensor(f"norm_psum_{number}", [P, 2, CH], F32))
        self.tallied = sem("norm_tallied")
        self.summed = sem("norm_summed")
        self.centred = sem("norm_centred")
        self.squared = sem("norm_squared")
        self.rooted = sem("norm_rooted")
        self.scaled = sem("norm_scaled")

    def start_pe(self, pe):
        pe.sem_inc(self.summed, 2)

    def start_dve(self, dve):
        dve.sem_inc(self.scaled, 1)

    def add(self, pool, n, i, tile, src):
        total = self.total[:, i, :]
        before = n * 2 * (KT - 1) + i * (KT - 1) + tile - 1
        if tile == 1:
            pool.wait_ge(self.summed, 2 * n + 1 + i)
            pool.tensor_tensor(total, src[:, 0, :], src[:, 1, :], ALU.add).then_inc(self.tallied, 1)
        else:
            pool.wait_ge(self.tallied, before)
            pool.tensor_tensor(total, total, src[:, tile, :], ALU.add).then_inc(self.tallied, 1)

    def pool_z(self, pool, n, z, tiles):
        for tile in tiles:
            pool.wait_ge(self.added, n * KT + tile + 1 + self.ahead)
            self.add(pool, n, 0, tile, z)

    def pool_squares(self, pool, n):
        for tile in range(1, KT):
            pool.wait_ge(self.squared, n * NPIECE + tile // PIECE + 1)
            self.add(pool, n, 1, tile, self.squares)

    def pe(self, pe, n, i):
        pe.wait_ge(self.tallied, (n * 2 + i + 1) * (KT - 1))
        pe.matmul(self.psum[:, i, :], self.ones, self.total[:, i, :], start=True, stop=True).then_inc(self.summed, 1)

    def pe_squares(self, pe, n):
        for tile in range(KT):
            pe.wait_ge(self.squared, n * NPIECE + tile // PIECE + 1)
            ins = pe.matmul(self.psum[:, 1, :], self.ones, self.squares[:, tile, :], start=(tile == 0), stop=(tile == KT - 1))
        ins.then_inc(self.summed, 1)

    def piece(self, z, i):
        return z[:, i * PIECE:(i + 1) * PIECE, :]

    def dve_centre(self, dve, n, z):
        dve.wait_ge(self.summed, n * 2 + 3)
        dve.tensor_scalar(self.mean[:, :], self.psum[:, 0, :], 1.0 / D, None, ALU.mult).then_inc(self.centred, 1)
        dve.wait_ge(self.centred, n * (NPIECE + 1) + 1)
        for i in range(NPIECE):
            dve.tensor_tensor(self.piece(z, i), self.piece(z, i), self.mean[:, :].unsqueeze(1).to_broadcast([P, PIECE, CH]),
                              ALU.subtract).then_inc(self.centred, 1)

    def act_square(self, act, n, z, i):
        act.wait_ge(self.centred, n * (NPIECE + 1) + i + 2)
        act.activation(self.piece(self.squares, i), self.piece(z, i), ACT.Square).then_inc(self.squared, 1)

    def act_root(self, act, n):
        act.wait_ge(self.summed, n * 2 + 4)
        act.wait_ge(self.scaled, n * (NPIECE + 1) + 1)
        act.activation(self.root[:, :], self.psum[:, 1, :], ACT.Sqrt, bias=self.eps[:, :], scale=1.0 / D).then_inc(self.rooted, 1)

    def dve_invert(self, dve, n):
        dve.wait_ge(self.rooted, n + 1)
        dve.reciprocal(self.root[:, :], self.root[:, :]).then_inc(self.scaled, 1)
        dve.wait_ge(self.scaled, n * (NPIECE + 1) + 2)

    def dve_scale(self, dve, z, i):
        dve.tensor_tensor(self.piece(z, i), self.piece(z, i), self.root[:, :].unsqueeze(1).to_broadcast([P, PIECE, CH]),
                          ALU.mult).then_inc(self.scaled, 1)

    def scaled_at(self, n, i):
        return n * (NPIECE + 1) + i + 3


def chunks(eng, chunk, slots, before, after):
    for c in range(before):
        chunk(c, c % slots, c, True)
    assert (NCH - before - after) % slots == 0
    with eng.Fori(0, (NCH - before - after) // slots) as it:
        for u in range(slots):
            chunk(it * slots + u + before, (u + before) % slots, before, True)
    for c in range(NCH - after, NCH):
        chunk(c, c % slots, before, c < NCH - 1)


ZS = 3


def mix(nc, x_chunks, att_o, att_l, att_inv, w_hi, w_lo, bias_o, perm, x1_hi, x1_lo):
    with ExitStack() as ctx:
        def sb(name, shape, dt):
            return ctx.enter_context(nc.sbuf_tensor(name, shape, dt))

        def sem(name):
            return ctx.enter_context(nc.semaphore(name))

        IR = 2
        att = sb("att", [P, KT, CH], F32)
        inv = sb("inv", [P, IR, CH], F32)
        a_hi = sb("a_hi", [P, KT, CH], F32R)
        a_lo = sb("a_lo", [P, KT, CH], F32R)
        z = sb("z3", [P, ZS, KT, CH], F32)
        x_hi = sb("x1_high", [P, KT, CH], F32R)
        bo = sb("bo", [P, KT], F32)
        rows = sb("rows3", [P, KT], I32)
        ones = sb("ones3", [P, P], F32)
        ps = ctx.enter_context(nc.psum_tensor("ps3", [P, 4, CH], F32))

        const_ready = sem("const_ready3")
        index_in = sem("index_in3")
        bias_in = sem("bias_in3")
        sums_in = sem("sums_in3")
        inverted = sem("inverted3")
        inverses_out = sem("inverses_out3")
        first_in = [sem(f"first_in{k}") for k in range(KT)]
        att_loaded = sem("att_loaded")
        inv_loaded = [sem(f"inv_loaded{i}") for i in range(IR)]
        rows_ready = sem("rows_ready3")
        x_loaded = sem("x_loaded3")
        first_divided = sem("first_divided")
        divided = sem("divided")
        a_hi_done = sem("a_hi_done")
        a_split = sem("a_split")
        a_used = sem("a_used")
        tile_ready = sem("tile_ready3")
        tile_used = sem("tile_used3")
        x_hi_done = sem("x1_hi_done")
        x_lo_done = sem("x1_lo_done")
        hi_stored = sem("hi_stored")
        lo_stored = sem("lo_stored")
        passed = sem("passed3")
        norm = Norm(nc, ctx, ones[:, :], 1, tile_used, 4)
        sums = norm.mean[:, :]
        block = ctx.enter_context(nc.Block())

        @block.sync
        def _(sp):
            def att_source(c, tiles):
                return att_o[ds(c // CPB, 1), tiles.start * P // HD:tiles.stop * P // HD, :, ds((c % CPB) * CH, CH)] \
                    .rearrange("b (k h) d t -> (b h d) k t", h=P // HD)

            def inv_source(c, k):
                return att_inv[ds(c // CPB, 1), k * P // HD:(k + 1) * P // HD, ds((c % CPB) * CH, CH)] \
                    .rearrange("b h t -> (b h) t").unsqueeze(1).to_broadcast([P // HD, HD, CH])

            def load_att(c):
                sp.dma_start(att[:, :, :], att_source(c, slice(0, KT))).then_inc(att_loaded, DMA)

            def load_inv(c):
                for k in range(KT):
                    sp.wait_ge(divided, (c - 1) * KT + k + 1)
                    sp.dma_start(inv[:, k % IR, :], inv_source(c, k)).then_inc(inv_loaded[k % IR], DMA)

            def store(c, slot):
                for done, x1, src, stored in ((x_hi_done, x1_hi, x_hi[:, :, :].bitcast(F32), hi_stored),
                                              (x_lo_done, x1_lo, z[:, slot, :, :], lo_stored)):
                    if stored is lo_stored:
                        sp.wait_ge(lo_stored, (c + 2) * NPIECE * DMA)
                    for i in range(NPIECE):
                        sp.wait_ge(done, c * NPIECE + i + 1)
                        sp.dma_start(x1[ds(c, 1), i * PIECE * P:(i + 1) * PIECE * P, :].rearrange("c (k p) t -> p (c k) t", p=P),
                                     norm.piece(src, i)).then_inc(stored, DMA)

            sp.dma_start(rows[:, :], perm).then_inc(index_in, DMA)
            for k in range(KT):
                sp.dma_start(norm.squares[:, k, :], inv_source(0, k)).then_inc(first_in[k], DMA)
                sp.dma_start(att[:, k:k + 1, :], att_source(0, slice(k, k + 1))).then_inc(first_in[k], DMA)
            sp.dma_start(sums, att_l[1].rearrange("h (q t) -> (h q) t", t=CH)).then_inc(sums_in, DMA)
            sp.sem_inc(hi_stored, NPIECE * DMA)
            sp.sem_inc(lo_stored, 2 * NPIECE * DMA)
            sp.wait_ge(inverted, 1)
            sp.dma_start(att_inv[1].rearrange("h (q t) -> (h q) t", t=CH), sums).then_inc(inverses_out, DMA)
            sp.wait_ge(inverses_out, DMA)

            def chunk(c, slot, past, more):
                if more:
                    sp.wait_ge(a_split, (c + 1) * KT)
                    load_att(c + 1)
                    load_inv(c + 1)
                if past:
                    store(c - 1, (slot - 1) % ZS)

            chunks(sp, chunk, ZS, 1, 1)
            store(NCH - 1, (NCH - 1) % ZS)
            sp.wait_ge(hi_stored, (NCH + 1) * NPIECE * DMA)
            sp.wait_ge(lo_stored, (NCH + 2) * NPIECE * DMA)

        @block.scalar
        def _(act):
            def split(n, z_of):
                for i in range(NPIECE):
                    if i == 0:
                        act.wait_ge(hi_stored, (n + 1) * NPIECE * DMA)
                    act.wait_ge(norm.scaled, norm.scaled_at(n, i))
                    act.activation(norm.piece(x_hi, i), norm.piece(z_of, i), ACT.Copy).then_inc(x_hi_done, 1)

            def chunk(c, slot, past, more):
                for k in range(KT):
                    act.wait_ge(divided if past else first_divided, k + 1 + ((c - 1) * KT + IR if past else 0))
                    act.wait_ge(a_used, c * KT + k + 1)
                    act.activation(a_hi[:, k, :], att[:, k, :], ACT.Copy).then_inc(a_hi_done, 1)
                if past:
                    behind = z[:, (slot - 1) % ZS, :, :]
                    for i in range(NPIECE):
                        norm.act_square(act, c - 1, behind, i)
                    norm.act_root(act, c - 1)
                    split(c - 1, behind)

            chunks(act, chunk, ZS, 1, 1)
            behind = z[:, (NCH - 1) % ZS, :, :]
            for i in range(NPIECE):
                norm.act_square(act, NCH - 1, behind, i)
            norm.act_root(act, NCH - 1)
            split(NCH - 1, behind)

        @block.gpsimd
        def _(pool):
            x_rows = x_chunks.rearrange("c d t -> (c d) t")

            def gather(c, slot):
                wait_apart(pool, rows_ready, c + 1, passed)
                for k in range(KT):
                    pool.indirect_dma_start(z[:, slot, k, :], None, x_rows,
                                            bass.IndirectOffsetOnAxis(ap=rows[:, k:k + 1].bitcast(U32), axis=0)).then_inc(x_loaded, DMA)

            pool.memset(ones[:, :], 1.0).then_inc(const_ready, 1)
            pool.memset(norm.eps[:, :], EPS).then_inc(const_ready, 1)
            pool.wait_ge(index_in, DMA)
            pool.sem_inc(rows_ready, 1)
            pool.wait_ge(first_in[KT - 1], 2 * DMA)
            gather(0, 0)
            for k in range(KT):
                pool.indirect_dma_start(bo[:, k:k + 1], None, bias_o,
                                        bass.IndirectOffsetOnAxis(ap=rows[:, k:k + 1].bitcast(U32), axis=0)).then_inc(bias_in, DMA)
            pool.wait_ge(bias_in, KT * DMA)

            def chunk(c, slot, past, more):
                if past:
                    norm.pool_z(pool, c - 1, z[:, (slot - 1) % ZS, :, :], [KT - 1])
                    norm.pool_squares(pool, c - 1)
                if more:
                    wait_apart(pool, x_loaded, (c + 1) * KT * DMA, passed)
                    pool.tensor_scalar(rows[:, :], rows[:, :], float(D), None, ALU.add).then_inc(rows_ready, 1)
                    pool.wait_ge(lo_stored, (c + 1) * NPIECE * DMA)
                    gather(c + 1, (slot + 1) % ZS)
                norm.pool_z(pool, c, z[:, slot, :, :], range(1, KT - 1))

            chunks(pool, chunk, ZS, 1, 1)
            norm.pool_z(pool, NCH - 1, z[:, (NCH - 1) % ZS, :, :], [KT - 1])

        @block.vector
        def _(dve):
            dve.sem_inc(tile_used, 4)
            dve.sem_inc(divided, IR)
            norm.start_dve(dve)

            def divide(c, tiles):
                for k in tiles:
                    if k == 0:
                        dve.wait_ge(att_loaded, c * DMA)
                    dve.wait_ge(inv_loaded[k % IR], ((c - 1) * (KT // IR) + k // IR + 1) * DMA)
                    dve.tensor_tensor(att[:, k, :], att[:, k, :], inv[:, k % IR, :], ALU.mult).then_inc(divided, 1)

            def add_tile(c, m, z_of):
                if m == 0:
                    dve.wait_ge(x_loaded, (c + 1) * KT * DMA)
                if m == KT - 1:
                    dve.wait_ge(a_used, (c + 2) * KT)
                else:
                    dve.wait_ge(tile_ready, c * (KT - 1) + m + 1)
                dve.scalar_tensor_tensor(out=z_of[:, m, :], in0=ps[:, m % 4, :], scalar=bo[:, m:m + 1],
                                         in1=z_of[:, m, :], op0=ALU.add, op1=ALU.add).then_inc(tile_used, 1)

            def scale(n, z_of):
                norm.dve_invert(dve, n)
                for i in range(NPIECE):
                    norm.dve_scale(dve, z_of, i)

            def split(n, z_of, pieces):
                for i in pieces:
                    dve.wait_ge(x_hi_done, n * NPIECE + i + 1)
                    dve.tensor_tensor(norm.piece(z_of, i), norm.piece(z_of, i), norm.piece(x_hi, i).bitcast(F32),
                                      ALU.subtract).then_inc(x_lo_done, 1)

            for k in range(KT):
                dve.wait_ge(first_in[k], 2 * DMA)
                dve.tensor_tensor(att[:, k, :], att[:, k, :], norm.squares[:, k, :], ALU.mult).then_inc(first_divided, 1)

            def chunk(c, slot, past, more):
                behind = z[:, (slot - 1) % ZS, :, :]
                for k in range(KT):
                    dve.wait_ge(a_hi_done, c * KT + k + 1)
                    dve.tensor_tensor(a_lo[:, k, :], att[:, k, :], a_hi[:, k, :].bitcast(F32), ALU.subtract).then_inc(a_split, 1)
                if past:
                    add_tile(c - 1, KT - 1, behind)
                else:
                    dve.wait_ge(sums_in, DMA)
                    dve.reciprocal(sums, sums).then_inc(inverted, 1)
                    dve.wait_ge(bias_in, KT * DMA)
                for m in range(KT - 1):
                    add_tile(c, m, z[:, slot, :, :])
                    if past and m == 0:
                        norm.dve_centre(dve, c - 1, behind)
                    if more and 2 <= m < 6:
                        divide(c + 1, (2 * m - 4, 2 * m - 3))
                    if past and m == 3:
                        scale(c - 1, behind)
                    if past and m >= 5:
                        split(c - 1, behind, (0, 1) if m == 5 else (2, 3))

            chunks(dve, chunk, ZS, 1, 1)
            behind = z[:, (NCH - 1) % ZS, :, :]
            add_tile(NCH - 1, KT - 1, behind)
            norm.dve_centre(dve, NCH - 1, behind)
            scale(NCH - 1, behind)
            split(NCH - 1, behind, range(NPIECE))

        @block.tensor
        def _(pe):
            norm.start_pe(pe)
            pe.sem_inc(a_used, KT)
            pe.wait_ge(const_ready, 2)

            def chunk(c, slot, past, more):
                for m in range(KT):
                    pe.wait_ge(tile_used, c * KT + m + 1)
                    for k in range(KT):
                        if m == 0:
                            pe.wait_ge(a_split, c * KT + k + 1)
                        for i, (w, a) in enumerate(((w_hi, a_hi), (w_hi, a_lo), (w_lo, a_hi))):
                            ins = pe.matmul(ps[:, m % 4, :], w[:, k, m * P:(m + 1) * P], a[:, k, :],
                                            start=(k == 0 and i == 0), stop=(k == KT - 1 and i == 2))
                        if m == KT - 1:
                            ins.then_inc(a_used, 1)
                        elif k == KT - 1:
                            ins.then_inc(tile_ready, 1)
                        if past and (m, k) == (1, 2):
                            norm.pe(pe, c - 1, 0)
                        if past and (m, k) == (3, KT - 1):
                            norm.pe(pe, c - 1, 1)

            chunks(pe, chunk, 1, 1, 0)
            norm.pe(pe, NCH - 1, 0)
            norm.pe_squares(pe, NCH - 1)


def feed(nc, x1_hi, x1_lo, perm, up, down, eye_pair, out):
    with ExitStack() as ctx:
        def sb(name, shape, dt):
            return ctx.enter_context(nc.sbuf_tensor(name, shape, dt))

        def sem(name):
            return ctx.enter_context(nc.semaphore(name))

        MT = FM // P
        NP2 = FH // 2
        GROUPS = 4
        HPG = FH // GROUPS
        t_st = sb("t_st", [P, 2, FH, CH], F32R)
        up_hi = sb("up_hi", [P, FH, FM], F32R)
        up_lo = sb("up_lo", [P, FH, FM], F32R)
        w_dn = sb("w_dn", [P, FH, MT, FD], F32)
        eyes_in = sb("eyes_in", [P, 2, P], F32)
        eyes = sb("eyes", [P, 2, P], F32R)
        act_out = sb("act_out", [P, 4, MT, CH], F32)
        z = sb("z4", [P, ZS, KT, CH], F32)
        rows = sb("rows4", [P, KT], I32)
        ones = sb("ones4", [P, P], F32)
        ps_u = ctx.enter_context(nc.psum_tensor("ps_u", [P, 2, MT, CH], F32))
        ps_d = ctx.enter_context(nc.psum_tensor("ps_d", [P, 2, CH], F32))

        const_ready = sem("const_ready4")
        index_in = sem("index_in4")
        up_loaded = [sem(f"up_loaded{g}") for g in range(GROUPS)]
        eyes_loaded = sem("eyes_loaded")
        eyes_ready = sem("eyes_ready")
        down_in = sem("down_in")
        up_hi_done = sem("up_hi_done")
        up_split = sem("up_split")
        t_loaded = [[sem(f"t_loaded{i}_{g}") for g in range(GROUPS)] for i in range(2)]
        up_ready = sem("up_ready")
        gelu_done = sem("gelu_done")
        down_ready = sem("down_ready")
        z_added = sem("z_added")
        rows_ready = sem("rows_ready4")
        stored = sem("stored4")
        scattered = sem("scattered")
        passed = sem("passed4")
        norm = Norm(nc, ctx, ones[:, :], 2, z_added, 2)
        up_in = norm.squares[:, :, :].rearrange("p a c -> p (a c)").rearrange("p (h m) -> p h m", h=FH)
        block = ctx.enter_context(nc.Block())
        out_rows = out.rearrange("c d t -> (c d) t")

        def heads(g):
            return slice(g * HPG, (g + 1) * HPG)

        @block.sync
        def _(sp):
            def load(c, slot, groups=range(GROUPS)):
                for g in groups:
                    for half, src in enumerate((x1_hi, x1_lo)):
                        sp.dma_start(t_st[half * FD:(half + 1) * FD, slot, heads(g), :].bitcast(F32),
                                     src[ds(c, 1), heads(g).start * FD:heads(g).stop * FD, :]
                                     .rearrange("c (h d) t -> d (c h) t", d=FD)).then_inc(t_loaded[slot][g], DMA)

            for g in range(GROUPS):
                for half in range(2):
                    sp.dma_start(up_in[half * FD:(half + 1) * FD, heads(g), :], up[:, heads(g), :]).then_inc(up_loaded[g], DMA)
                load(0, 0, [g])
                if g == 0:
                    sp.dma_start(eyes_in[:, :, :], eye_pair).then_inc(eyes_loaded, DMA)
                    sp.dma_start(w_dn[:, :, :, :], down).then_inc(down_in, DMA)
            sp.dma_start(rows[:, :], perm).then_inc(index_in, DMA)
            load(1, 1)
            with sp.Fori(0, (NCH - 2) // 2) as it:
                for slot in range(2):
                    c = it * 2 + slot + 2
                    sp.wait_ge(down_ready, (c - 1) * NP2 + 2)
                    load(c, slot)

        @block.scalar
        def _(act):
            act.sem_inc(gelu_done, 2)

            def split_up(g):
                act.wait_ge(up_loaded[g], 2 * DMA)
                act.activation(up_hi[:, heads(g), :], up_in[:, heads(g), :], ACT.Copy).then_inc(up_hi_done, 1)

            split_up(0)

            def chunk(c, slot, past, more):
                behind = z[:, (slot - 1) % ZS, :, :]
                for h in range(FH):
                    act.wait_ge(up_ready, c * FH + h + 1)
                    act.wait_ge(down_ready, c * NP2 + h // 2 + 1)
                    act.activation(act_out[:, h % 4, :, :], ps_u[:, h % 2, :, :], ACT.Gelu).then_inc(gelu_done, 1)
                    if past == 0 and h == 1:
                        act.wait_ge(eyes_loaded, DMA)
                        act.activation(eyes[:, :, :], eyes_in[:, :, :], ACT.Copy).then_inc(eyes_ready, 1)
                    if past == 0 and h % HPG == 1 and h // HPG + 1 < GROUPS:
                        split_up(h // HPG + 1)
                    if past and h in (3, 5, 7, 9):
                        norm.act_square(act, c - 1, behind, (h - 3) // 2)
                    if past and h == 11:
                        norm.act_root(act, c - 1)

            chunks(act, chunk, ZS, 2, 0)
            for i in range(NPIECE):
                norm.act_square(act, NCH - 1, z[:, (NCH - 1) % ZS, :, :], i)
            norm.act_root(act, NCH - 1)

        @block.gpsimd
        def _(pool):
            pool.memset(ones[:, :], 1.0).then_inc(const_ready, 1)
            pool.memset(norm.eps[:, :], EPS).then_inc(const_ready, 1)
            pool.sem_inc(scattered, ZS)
            pool.wait_ge(index_in, DMA)
            pool.sem_inc(rows_ready, 1)

            def scatter(n, slot):
                for k in range(KT):
                    if k == 0:
                        pool.wait_ge(rows_ready, n + 1)
                    if k % PIECE == 0:
                        wait_apart(pool, norm.scaled, norm.scaled_at(n, k // PIECE), passed)
                    pool.indirect_dma_start(out_rows, bass.IndirectOffsetOnAxis(ap=rows[:, k:k + 1].bitcast(U32), axis=0),
                                            z[:, slot, k, :], None).then_inc(stored, DMA)

            def scattered_chunk(n, more):
                wait_apart(pool, stored, (n + 1) * KT * DMA, scattered)
                if more:
                    pool.tensor_scalar(rows[:, :], rows[:, :], float(D), None, ALU.add).then_inc(rows_ready, 1)

            def chunk(c, slot, past, more):
                if past:
                    norm.pool_z(pool, c - 1, z[:, (slot - 1) % ZS, :, :], [KT - 1])
                    norm.pool_squares(pool, c - 1)
                if past == 2:
                    scatter(c - 2, (slot - 2) % ZS)
                norm.pool_z(pool, c, z[:, slot, :, :], range(1, KT - 1))
                if past == 2:
                    scattered_chunk(c - 2, True)

            chunks(pool, chunk, ZS, 2, 0)
            norm.pool_z(pool, NCH - 1, z[:, (NCH - 1) % ZS, :, :], [KT - 1])
            for n in (NCH - 2, NCH - 1):
                scatter(n, n % ZS)
                scattered_chunk(n, n < NCH - 1)

        @block.vector
        def _(dve):
            dve.sem_inc(z_added, 2)
            norm.start_dve(dve)

            def split_up(g):
                dve.wait_ge(up_hi_done, g + 1)
                dve.tensor_tensor(up_lo[:, heads(g), :], up_in[:, heads(g), :], up_hi[:, heads(g), :].bitcast(F32),
                                  ALU.subtract).then_inc(up_split, 1)

            split_up(0)
            split_up(1)

            def copy_tile(c, i, z_of):
                dve.wait_ge(down_ready, c * NP2 + i + 3)
                dve.tensor_copy(z_of[:, i, :], ps_d[:, i % 2, :]).then_inc(z_added, 1)

            def chunk(c, slot, past, more):
                behind = z[:, (slot - 1) % ZS, :, :]
                dve.wait_ge(scattered, c + 1)
                if past:
                    copy_tile(c - 1, NP2 - 1, behind)
                    norm.dve_centre(dve, c - 1, behind)
                for i in range(NP2 - 1):
                    if past == 0 and i in (2, 4):
                        split_up(i // 2 + 1)
                    copy_tile(c, i, z[:, slot, :, :])
                    if past and i >= 4:
                        if i == 4:
                            norm.dve_invert(dve, c - 1)
                        for piece in ((0,), (1, 2), (3,))[i - 4]:
                            norm.dve_scale(dve, behind, piece)

            chunks(dve, chunk, ZS, 2, 0)
            behind = z[:, (NCH - 1) % ZS, :, :]
            copy_tile(NCH - 1, NP2 - 1, behind)
            norm.dve_centre(dve, NCH - 1, behind)
            norm.dve_invert(dve, NCH - 1)
            for i in range(NPIECE):
                norm.dve_scale(dve, behind, i)

        @block.tensor
        def _(pe):
            pe.sem_inc(down_ready, 2)
            norm.start_pe(pe)

            def down_pair(c, i, slot):
                pe.wait_ge(gelu_done, c * FH + 2 * i + 4)
                pe.wait_ge(z_added, c * NP2 + i + 1)
                for half in range(2):
                    pe.matmul(ps_d[:, i % 2, :], eyes[:, half, :], t_st[:, slot, 2 * i + half, :],
                              start=(half == 0), stop=False, skip_group_check=True)
                for m in range(MT):
                    for half in range(2):
                        h = 2 * i + half
                        ins = pe.matmul(ps_d[half * FD:(half + 1) * FD, i % 2, :], w_dn[:, h, m, :], act_out[:, h % 4, m, :],
                                        start=False, stop=(m == MT - 1), skip_group_check=True)
                ins.then_inc(down_ready, 1)

            def chunk(c, slot, past, more):
                for h in range(FH):
                    if h % HPG == 0:
                        pe.wait_ge(t_loaded[slot][h // HPG], (c // 2 + 1) * 2 * DMA)
                        if past == 0:
                            pe.wait_ge(up_split, h // HPG + 1)
                    pe.wait_ge(gelu_done, c * FH + h + 1)
                    for m in range(MT):
                        for i, w in enumerate((up_hi, up_lo)):
                            ins = pe.matmul(ps_u[:, h % 2, m, :], w[:, h, m * P:(m + 1) * P], t_st[:, slot, h, :], start=(i == 0), stop=(i == 1))
                    ins.then_inc(up_ready, 1)
                    if past == 0 and h == 3:
                        pe.wait_ge(const_ready, 2)
                        pe.wait_ge(eyes_ready, 1)
                        pe.wait_ge(down_in, DMA)
                    if h == 1 and past:
                        down_pair(c - 1, NP2 - 1, 1 - slot)
                    if h % 2 == 1 and h > 1:
                        down_pair(c, h // 2 - 1, slot)
                    if h == 3 and past:
                        norm.pe(pe, c - 1, 0)
                    if h == 11 and past:
                        norm.pe(pe, c - 1, 1)

            chunks(pe, chunk, 2, 2, 0)
            down_pair(NCH - 1, NP2 - 1, (NCH - 1) % 2)
            norm.pe(pe, NCH - 1, 0)
            norm.pe_squares(pe, NCH - 1)


def build(nc, arrays, phases=4):
    def given(name):
        a = arrays[name]
        return nc.dram_tensor(name, a.shape, mybir.dt.from_np(a.dtype), kind="ExternalInput").ap()

    def kept(name, shape):
        return nc.dram_tensor(name, shape, F32, kind="Internal").ap()

    g = {name: given(name) for name in arrays}
    out = nc.dram_tensor("out_0_dram", [NCH, D, CH], F32, kind="ExternalOutput").ap()
    qk_halves = kept("qk_halves", [B, H + KV, 4, HALF, S])
    v_keys = kept("v_keys", [B, KV, P, S // P, HD])
    att_o = kept("att_o", [B, H, HD, S])
    att_l = kept("att_l", [B, H, S])
    att_inv = kept("att_inv", [B, H, S])
    x1_hi = kept("x1_hi", [NCH, D, CH])
    x1_lo = kept("x1_lo", [NCH, D, CH])
    project(nc, g["x_chunks"], g["wqkvT"], g["bias_qk"], g["bias_v"], g["cos"], g["sin"], qk_halves, v_keys)
    with ExitStack() as ctx:
        wo_hi = ctx.enter_context(nc.sbuf_tensor("wo_hi", [P, KT, D], F32R))
        wo_lo = ctx.enter_context(nc.sbuf_tensor("wo_lo", [P, KT, D], F32R))
        if phases >= 2:
            attend(nc, qk_halves, v_keys, g["identity"], g["w_o"], g["perm"], wo_hi, wo_lo, att_o, att_l, att_inv)
        if phases >= 3:
            mix(nc, g["x_chunks"], att_o, att_l, att_inv, wo_hi, wo_lo, g["bias_o"], g["perm"], x1_hi, x1_lo)
    if phases >= 4:
        feed(nc, x1_hi, x1_lo, g["perm"], g["up"], g["down"], g["eye_pair"], out)


def host_layout(L0_attn_x, L0_attn_w_qkv, L0_attn_b_qkv, L0_attn_w_o, L0_attn_b_o, L0_ffn_up, L0_ffn_down, L0_ffn_perm):
    c = np.ascontiguousarray
    rows = np.arange((H + KV) * HD).reshape(QK_PAIRS, HPT, HALF, 2).transpose(0, 3, 1, 2).reshape(-1)
    perm = np.asarray(L0_ffn_perm)
    order = np.concatenate([rows, np.arange((H + KV) * HD, (H + 2 * KV) * HD)])
    inv_freq = np.float32(1.0) / np.power(np.float32(10000.0), np.arange(0, HD, 2, dtype=np.float32) / np.float32(HD))
    angle = np.arange(S, dtype=np.float32)[None, :] * inv_freq[:, None]
    return {
        "x_chunks": c(np.asarray(L0_attn_x).reshape(NCH, CH, D).transpose(0, 2, 1)),
        "wqkvT": c(np.asarray(L0_attn_w_qkv)[order].T),
        "bias_qk": c(np.asarray(L0_attn_b_qkv)[rows].reshape(2 * QK_PAIRS, P).T),
        "bias_v": c(np.asarray(L0_attn_b_qkv)[(H + KV) * HD:]),
        "w_o": c(np.asarray(L0_attn_w_o)),
        "bias_o": c(np.asarray(L0_attn_b_o).reshape(D, 1)),
        "up": c(np.asarray(L0_ffn_up).transpose(1, 0, 2)),
        "down": c(np.asarray(L0_ffn_down).reshape(FH, FM // P, P, FD).transpose(2, 0, 1, 3)),
        "perm": c(perm.reshape(KT, P).T),
        "cos": c(np.tile(np.cos(angle.astype(np.float64)).astype(np.float32), (HPT, 1))),
        "sin": c(np.tile(np.sin(angle.astype(np.float64)).astype(np.float32), (HPT, 1))),
        "identity": np.eye(P, dtype=np.float32),
        "eye_pair": c(np.tile(np.eye(P, dtype=np.float32).reshape(P // FD, FD, P).transpose(1, 0, 2), (P // FD, 1, 1))),
    }


def result(chunks):
    return np.ascontiguousarray(chunks.transpose(0, 2, 1).reshape(B, S, D))


def kernel(**inputs):
    import concourse.bacc as bacc
    from concourse.bass_utils import run_bass_kernel_spmd

    arrays = host_layout(**{name: np.asarray(a) for name, a in inputs.items()})
    nc = bacc.Bacc("TRN2", target_bir_lowering=False, num_devices=1)
    build(nc, arrays)
    r = run_bass_kernel_spmd(nc, [arrays], core_ids=[0])
    return result(r.results[0]["out_0_dram"])
```
